# Optimizing a Trainium2 kernel written in Bass

```python
import numpy as np
import jax
import jax.numpy as jnp

def _softmax(x, axis=-1):
    return jax.nn.softmax(x, axis=axis)

def _gelu(x):
    return jax.nn.gelu(x, approximate=True)

def _silu(x):
    return jax.nn.silu(x)

def _sigmoid(x):
    return jax.nn.sigmoid(x)

def _layernorm(x, axis=-1, eps=1e-05):
    m = jnp.mean(x, axis=axis, keepdims=True)
    v = jnp.var(x, axis=axis, keepdims=True)
    return (x - m) / jnp.sqrt(v + eps)

def _scatter_add(tgt, idx, src, axis=0):
    return tgt.at[idx].add(src)

def _segment_sum(src, seg, n):
    return jax.ops.segment_sum(src, seg, n)
kernel_name = 'mk_gnn_ffn_d2_gnn_r8_db4807'

def setup_inputs(seed: int=0):
    np.random.seed(seed)
    _w = jnp.asarray

    def _rec_inputs():
        import jax
        import jax.numpy as jnp
        _gk = jax.random.key(seed)
        x = -0.0002117 + 1 * jax.random.normal(jax.random.fold_in(_gk, 1), (12500, 256), jnp.float32)
        _s = jax.random.randint(jax.random.fold_in(_gk, 2), (100000,), 0, 12500, jnp.int32)
        _d = jax.random.randint(jax.random.fold_in(_gk, 3), (100000,), 0, 12500, jnp.int32)
        _loop = jnp.arange(12500, dtype=jnp.int32)
        src = jnp.concatenate([_s, _d, _loop])
        dst = jnp.concatenate([_d, _s, _loop])
        _o = jnp.argsort(dst, stable=True)
        src = src[_o]
        dst = dst[_o]
        return (x, src, dst)
    x, src, dst = _rec_inputs()

    def _L0_gnn_setup():
        import jax, jax.numpy as jnp
        import numpy as np
        N = 12500
        E = 200000
        H, F_IN, F_OUT = (8, 256, 32)
        key = jax.random.key(seed)
        k1, k2, k3, k4, k5 = jax.random.split(key, 5)
        x = jax.random.normal(k1, (N, F_IN), dtype=jnp.float32)
        edge_index = jax.random.randint(k2, (2, E), 0, N, dtype=jnp.int64)
        W = jax.random.normal(k3, (H, F_IN, F_OUT), dtype=jnp.float32) * (1.0 / np.sqrt(F_IN))
        a_src = jax.random.normal(k4, (H, F_OUT, 1), dtype=jnp.float32) * 0.1
        a_dst = jax.random.normal(k5, (H, F_OUT, 1), dtype=jnp.float32) * 0.1
        return {'x': x, 'edge_index': edge_index, 'W': W, 'a_src': a_src, 'a_dst': a_dst}
    _L0_gnn_all = _L0_gnn_setup()
    _L0_gnn_in = {k: v for k, v in _L0_gnn_all.items() if k in ('W', 'a_src', 'a_dst')}
    del _L0_gnn_all

    def _L0_ffn_setup():
        import jax, jax.numpy as jnp
        import numpy as np
        BN_EPS = 0.001

        def _bn(h, g, b, m, v):
            return g * (h - m) * jax.lax.rsqrt(v + BN_EPS) + b
        key = jax.random.key(seed)
        ks = jax.random.split(key, 8)
        B, F, Df = (256, 64, 256)
        E, H, D = (8, 256, 256)
        s1 = 1.0 / np.sqrt(Df)
        s2 = 1.0 / np.sqrt(H)
        return {'x': jax.random.normal(ks[0], (B, F, Df), jnp.float32), 'Wr': jax.random.normal(ks[1], (Df, E), jnp.float32) * s1, 'br': jnp.zeros((E,), jnp.float32), 'W1': jax.random.normal(ks[2], (E, Df, H), jnp.float32) * s1, 'b1': jnp.zeros((E, H), jnp.float32), 'g1': jnp.ones((E, H), jnp.float32), 'be1': jnp.zeros((E, H), jnp.float32), 'm1': jnp.zeros((E, H), jnp.float32), 'v1': jnp.ones((E, H), jnp.float32), 'W2': jax.random.normal(ks[3], (E, H, H), jnp.float32) * s2, 'b2': jnp.zeros((E, H), jnp.float32), 'g2': jnp.ones((E, H), jnp.float32), 'be2': jnp.zeros((E, H), jnp.float32), 'm2': jnp.zeros((E, H), jnp.float32), 'v2': jnp.ones((E, H), jnp.float32), 'Wo': jax.random.normal(ks[4], (E, H, D), jnp.float32) * s2, 'bo': jnp.zeros((E, D), jnp.float32)}
    _L0_ffn_all = _L0_ffn_setup()
    _L0_ffn_in = {k: v for k, v in _L0_ffn_all.items() if k in ('Wr', 'br', 'W1', 'b1', 'g1', 'be1', 'm1', 'v1', 'W2', 'b2', 'g2', 'be2', 'm2', 'v2', 'Wo', 'bo')}
    del _L0_ffn_all

    def _L1_gnn_setup():
        import jax, jax.numpy as jnp
        import numpy as np
        N_NODES = 1250
        N_EDGES = 40000
        D_IN = 256
        D_OUT = 256
        key = jax.random.key(seed)
        k1, k2, k3, k4 = jax.random.split(key, 4)
        x = jax.random.normal(k1, (N_NODES, D_IN), dtype=jnp.float32)
        edge_index = jax.random.randint(k2, (2, N_EDGES), 0, N_NODES, dtype=jnp.int64)
        weight = jax.random.normal(k3, (2 * D_IN, D_OUT), dtype=jnp.float32) / np.sqrt(2 * D_IN)
        bias = jax.random.normal(k4, (D_OUT,), dtype=jnp.float32)
        return {'x': x, 'edge_index': edge_index, 'weight': weight, 'bias': bias}
    _L1_gnn_all = _L1_gnn_setup()
    _L1_gnn_in = {k: v for k, v in _L1_gnn_all.items() if k in ('weight', 'bias')}
    del _L1_gnn_all

    def _L1_ffn_setup():
        import math
        import jax, jax.numpy as jnp
        import numpy as np
        CAPACITY_FACTOR = 1.25
        key = jax.random.key(seed)
        ks = jax.random.split(key, 5)
        B, L, D, F, E = (8, 1024, 256, 1024, 8)
        h = jax.random.normal(ks[0], (B, L, D), dtype=jnp.float32)
        gate_w = jax.random.normal(ks[1], (D, E), dtype=jnp.float32) * 0.02
        gate_b = jnp.zeros((E,), dtype=jnp.float32)
        w1 = jax.random.normal(ks[2], (E, D, F), dtype=jnp.float32) * (1.0 / math.sqrt(D))
        b1 = jnp.zeros((E, F), dtype=jnp.float32)
        w2 = jax.random.normal(ks[3], (E, F, D), dtype=jnp.float32) * (1.0 / math.sqrt(F))
        b2 = jnp.zeros((E, D), dtype=jnp.float32)
        return {'h': h, 'gate_w': gate_w, 'gate_b': gate_b, 'w1': w1, 'b1': b1, 'w2': w2, 'b2': b2}
    _L1_ffn_all = _L1_ffn_setup()
    _L1_ffn_in = {k: v for k, v in _L1_ffn_all.items() if k in ('gate_w', 'gate_b', 'w1', 'b1', 'w2', 'b2')}
    del _L1_ffn_all
    return {'x': x, 'src': src, 'dst': dst, 'L0_gnn_W': _L0_gnn_in['W'], 'L0_gnn_a_src': _L0_gnn_in['a_src'], 'L0_gnn_a_dst': _L0_gnn_in['a_dst'], 'L0_ffn_Wr': _L0_ffn_in['Wr'], 'L0_ffn_br': _L0_ffn_in['br'], 'L0_ffn_W1': _L0_ffn_in['W1'], 'L0_ffn_b1': _L0_ffn_in['b1'], 'L0_ffn_g1': _L0_ffn_in['g1'], 'L0_ffn_be1': _L0_ffn_in['be1'], 'L0_ffn_m1': _L0_ffn_in['m1'], 'L0_ffn_v1': _L0_ffn_in['v1'], 'L0_ffn_W2': _L0_ffn_in['W2'], 'L0_ffn_b2': _L0_ffn_in['b2'], 'L0_ffn_g2': _L0_ffn_in['g2'], 'L0_ffn_be2': _L0_ffn_in['be2'], 'L0_ffn_m2': _L0_ffn_in['m2'], 'L0_ffn_v2': _L0_ffn_in['v2'], 'L0_ffn_Wo': _L0_ffn_in['Wo'], 'L0_ffn_bo': _L0_ffn_in['bo'], 'L1_gnn_weight': _L1_gnn_in['weight'], 'L1_gnn_bias': _L1_gnn_in['bias'], 'L1_ffn_gate_w': _L1_ffn_in['gate_w'], 'L1_ffn_gate_b': _L1_ffn_in['gate_b'], 'L1_ffn_w1': _L1_ffn_in['w1'], 'L1_ffn_b1': _L1_ffn_in['b1'], 'L1_ffn_w2': _L1_ffn_in['w2'], 'L1_ffn_b2': _L1_ffn_in['b2']}

def reference(x, src, dst, L0_gnn_W, L0_gnn_a_src, L0_gnn_a_dst, L0_ffn_Wr, L0_ffn_br, L0_ffn_W1, L0_ffn_b1, L0_ffn_g1, L0_ffn_be1, L0_ffn_m1, L0_ffn_v1, L0_ffn_W2, L0_ffn_b2, L0_ffn_g2, L0_ffn_be2, L0_ffn_m2, L0_ffn_v2, L0_ffn_Wo, L0_ffn_bo, L1_gnn_weight, L1_gnn_bias, L1_ffn_gate_w, L1_ffn_gate_b, L1_ffn_w1, L1_ffn_b1, L1_ffn_w2, L1_ffn_b2):
    import jax
    import jax.numpy as jnp

    def _L0_gnn_ref(x, edge_index, W, a_src, a_dst):
        import jax, jax.numpy as jnp
        import numpy as np
        N = 12500
        E = 200000
        H, F_IN, F_OUT = (8, 256, 32)
        src, dst = (edge_index[0], edge_index[1])
        h = jnp.einsum('ni,hio->hno', x, W)
        attn_src = jnp.einsum('hno,ho->hn', h, a_src[..., 0])
        attn_dst = jnp.einsum('hno,ho->hn', h, a_dst[..., 0])
        edge_attn = jax.nn.leaky_relu(attn_src[:, src] + attn_dst[:, dst], negative_slope=0.2)
        edge_attn_exp = jnp.exp(edge_attn - jnp.max(edge_attn))
        attn_sum = jax.ops.segment_sum(edge_attn_exp.T, dst, num_segments=N)
        attn_norm = edge_attn_exp / (attn_sum[dst].T + 1e-10)
        weighted_h = attn_norm[..., None] * h[:, src]
        out = jax.ops.segment_sum(weighted_h.transpose(1, 0, 2), dst, num_segments=N)
        out = out.reshape(N, H * F_OUT)
        return out + x

    def _L0_ffn_ref(x, Wr, br, W1, b1, g1, be1, m1, v1, W2, b2, g2, be2, m2, v2, Wo, bo):
        import jax, jax.numpy as jnp
        import numpy as np
        BN_EPS = 0.001

        def _bn(h, g, b, m, v):
            return g * (h - m) * jax.lax.rsqrt(v + BN_EPS) + b
        feat = jnp.mean(x, axis=0)
        w = jax.nn.softmax(feat @ Wr + br, axis=-1)
        h = jnp.einsum('bfd,edh->bfeh', x, W1) + b1
        h = jax.nn.relu(_bn(h, g1, be1, m1, v1))
        h = jnp.einsum('bfeh,ehk->bfek', h, W2) + b2
        h = jax.nn.relu(_bn(h, g2, be2, m2, v2))
        y = jnp.einsum('bfeh,ehd->bfed', h, Wo) + bo
        return jnp.einsum('bfed,fe->bfd', y, w)

    def _L1_gnn_ref(x, edge_index, weight, bias):
        import jax, jax.numpy as jnp
        import numpy as np
        N_NODES = 1250
        N_EDGES = 40000
        D_IN = 256
        D_OUT = 256
        n = x.shape[0]
        src, dst = (edge_index[0], edge_index[1])
        summed = jax.ops.segment_sum(x[src], dst, num_segments=n)
        deg = jax.ops.segment_sum(jnp.ones_like(src, dtype=x.dtype), dst, num_segments=n)
        agg = summed / jnp.maximum(deg, 1.0)[:, None]
        out = jnp.concatenate([x, agg], axis=-1) @ weight
        out = out / jnp.linalg.norm(out, axis=-1, keepdims=True)
        return out + bias

    def _L1_ffn_ref(h, gate_w, gate_b, w1, b1, w2, b2):
        import math
        import jax, jax.numpy as jnp
        import numpy as np
        CAPACITY_FACTOR = 1.25
        B, L, D = h.shape
        E = gate_w.shape[1]
        T = B * L
        C = max(1, math.ceil(CAPACITY_FACTOR * T / E))
        x = h.reshape(T, D)
        logits = x @ gate_w + gate_b
        probs = jax.nn.softmax(logits, axis=-1)
        idx = jnp.argmax(probs, axis=-1)
        prb = jnp.take_along_axis(probs, idx[:, None], axis=1)[:, 0]
        one_hot = jax.nn.one_hot(idx, E, dtype=jnp.float32)
        pos = (jnp.cumsum(one_hot, axis=0) * one_hot).sum(-1).astype(jnp.int32) - 1
        kept = pos < C
        pos_safe = jnp.where(kept, pos, C)
        buf = jnp.zeros((E, C, D), dtype=h.dtype).at[idx, pos_safe].set(x, mode='drop')
        hmid = jax.nn.relu(jnp.einsum('ecd,edf->ecf', buf, w1) + b1[:, None, :])
        ybuf = jnp.einsum('ecf,efd->ecd', hmid, w2) + b2[:, None, :]
        pos_g = jnp.minimum(pos, C - 1)
        y_tok = ybuf[idx, pos_g] * (prb * kept)[:, None]
        y = y_tok.reshape(B, L, D)
        y = jnp.nan_to_num(y, nan=0.0, posinf=10000.0, neginf=-10000.0)
        return y
    edge_index = jnp.stack([src, dst])
    x = x + _L0_gnn_ref(_layernorm(x, axis=-1), edge_index, L0_gnn_W, L0_gnn_a_src, L0_gnn_a_dst)
    x = x + _L0_ffn_ref(_layernorm(x, axis=-1)[None], L0_ffn_Wr, L0_ffn_br, L0_ffn_W1, L0_ffn_b1, L0_ffn_g1, L0_ffn_be1, L0_ffn_m1, L0_ffn_v1, L0_ffn_W2, L0_ffn_b2, L0_ffn_g2, L0_ffn_be2, L0_ffn_m2, L0_ffn_v2, L0_ffn_Wo, L0_ffn_bo)[0]
    x = x + _L1_gnn_ref(_layernorm(x, axis=-1), edge_index, L1_gnn_weight, L1_gnn_bias)
    x = x + _L1_ffn_ref(_layernorm(x, axis=-1)[None], L1_ffn_gate_w, L1_ffn_gate_b, L1_ffn_w1, L1_ffn_b1, L1_ffn_w2, L1_ffn_b2)[0]
    return x

_drawn_inputs = setup_inputs


def setup_inputs(seed=0):
    import zlib

    import numpy as np

    out = dict(_drawn_inputs(seed))
    spreads = {'L0_ffn_br': (0.0, 0.466),
     'L0_ffn_b1': (0.0, 0.595),
     'L0_ffn_g1': (1.0, 0.6),
     'L0_ffn_be1': (0.0, 0.617),
     'L0_ffn_m1': (0.0, 0.593),
     'L0_ffn_v1': (1.0, 0.6),
     'L0_ffn_b2': (0.0, 0.445),
     'L0_ffn_g2': (1.0, 0.598),
     'L0_ffn_be2': (0.0, 0.448),
     'L0_ffn_m2': (0.0, 0.454),
     'L0_ffn_v2': (1.0, 0.6),
     'L0_ffn_bo': (0.0, 0.348),
     'L1_ffn_gate_b': (0.0, 0.277),
     'L1_ffn_b1': (0.0, 0.8),
     'L1_ffn_b2': (0.0, 0.8)}
    factors = {'L0_gnn_a_dst': 2.983}
    for name, (base, spread) in spreads.items():
        noise = np.random.default_rng([zlib.crc32(name.encode()), seed]).standard_normal(out[name].shape)
        drawn = base * np.exp(spread * noise) if base else spread * noise
        out[name] = jnp.asarray(drawn.astype(out[name].dtype))
    for name, factor in factors.items():
        out[name] = (out[name] * factor).astype(out[name].dtype)
    return out
```

```python
import math
from contextlib import ExitStack

import concourse.bass as bass
from concourse import mybir

FP32 = mybir.dt.float32
BF16 = mybir.dt.bfloat16
F32R = mybir.dt.float32r
I32 = mybir.dt.int32
U32 = mybir.dt.uint32
ALU = mybir.AluOpType
ACT = mybir.ActivationFunctionType
AX = mybir.AxisListType
ADD, SUB, MUL, MAX, MIN = ALU.add, ALU.subtract, ALU.mult, ALU.max, ALU.min
REDUCE_MAX = bass.bass_isa.ReduceOp.max

P = 128
N = 12500
D = 256
KB = D // P
E = 212500
H = 8
HD = D // H
NX = 8
LN_EPS, BN_EPS, ATT_EPS = 1e-5, 1e-3, 1e-10
LEAK = 0.2

NT = -(-N // P)
TAIL = N - (NT - 1) * P
NP = NT * P
GT = 7
NG = NT // GT
assert NG * GT == NT and NG % 2 == 0

ET = -(-E // P)
ETAIL = E - (ET - 1) * P
RB = -(-ET // P)
CH = 6
HT = CH // 2
CE = CH * P
RING = 4
MINC = 2
PADR = -(-(CE * (MINC + RING) + P) // P)
EROWS = RB * P + PADR
NOWHERE = 1 << 14
VT = 128
HUGE = 1e30

NA = D + H
NV = NA + 1
ND = 2 * H + 1

FH = 1024
FB = FH // P
CAP = max(1, math.ceil(1.25 * N / NX))
TC = 512
CT = TC // P
SLOTS = -(-CAP // TC) * TC
GM = 2
FILL = -(-NX * SLOTS // (NT // GM * P))
XW = 2 * D + 2
FAR = 1 << 16
BIGGEST = 3.4028234663852886e38
NN_INF = 1e4


VOID = 16


def build(nc, a, out, scratch):
    top = ExitStack()
    with top:
        def sem(ctx, name, pool_dma=False):
            if pool_dma:
                return top.enter_context(nc.semaphore(name))
            one = ctx.enter_context(nc.semaphore(name))
            of_phase.append(one)
            return one

        of_phase = []

        def phase(program, *args):
            with ExitStack() as ctx:
                program(nc, *args, ctx, sem, sbuf, psum)
                with nc.Block() as block:
                    @block.gpsimd
                    def _(gp):
                        for one in of_phase:
                            gp.sem_clear(one)
                of_phase.clear()

        def sbuf(ctx, name, shape, dt=FP32):
            return ctx.enter_context(nc.sbuf_tensor(name, shape, dt))

        def psum(ctx, name, shape=(P, 512), dt=FP32):
            return ctx.enter_context(nc.psum_tensor(name, list(shape), dt))

        k = {}
        k["void"] = scratch["void"]
        k["void_rows"] = iter(range(VOID))
        k["ident"] = sbuf(top, "ident", [P, P])
        k["iota"] = sbuf(top, "iota", [P, P])
        k["zeros"] = sbuf(top, "zeros", [P, NV], BF16)
        k["visits"] = sbuf(top, "visits", [1, 2 * VT + 1], I32)
        k["node"] = sbuf(top, "node_rows", [P, NT, ND])
        k["amax"] = sbuf(top, "amax", [P, H])
        k["zmax"] = sbuf(top, "zmax", [P, CH * H])
        k["deg"] = sbuf(top, "deg", [P, NT])
        k["chunks"] = sbuf(top, "chunks", [1, NX], I32)
        phase(prepare, a, k, scratch)
        phase(project_attention, a, k, scratch)
        phase(attention_edges, k, scratch)
        phase(mixture, a, k, scratch)
        phase(mean_edges, k, scratch)
        phase(route, a, k, scratch, out)
        phase(experts, a, k, scratch, out)


def first_turn(eng, k, one, count=1):
    for _ in range(count):
        n = next(k["void_rows"])
        eng.dma_start(k["void"][n:n + 1, :], k["ident"][0:1, 0:16]).then_inc(one, 16)


def prepare(nc, a, k, scratch, ctx, sem, sbuf, psum):
    raw = {n: sbuf(ctx, f"raw_{n}", [P, RB, P], I32) for n in ("src", "dst")}
    pad = {n: sbuf(ctx, f"pad_{n}", [PADR, P], I32) for n in ("src", "dst")}
    dst_f = sbuf(ctx, "dst_f", [P, RB, P])
    iota_i = sbuf(ctx, "iota_i", [P, RB * P], I32)
    tile_no = sbuf(ctx, "tile_no", [P, RB * P])
    node0_i = sbuf(ctx, "node0_i", [P, 2], I32)
    node0 = sbuf(ctx, "node0", [P, 2])
    ends = sbuf(ctx, "ends", [P, 2, RB])
    lows = sbuf(ctx, "lows", [P, RB * P])
    highs = sbuf(ctx, "highs", [P, RB * P])
    v1 = sbuf(ctx, "v1", [P, RB * P])
    v2 = sbuf(ctx, "v2", [P, RB * P])
    tiles = sbuf(ctx, "tiles", [P, 2])
    tiles_i = sbuf(ctx, "tiles_i", [P, 2], I32)
    edge_i = sbuf(ctx, "edge_i", [P, 2, P], I32)
    edge = sbuf(ctx, "edge", [P, 2, P])
    in1 = sbuf(ctx, "in1", [P, 2, P])
    in2 = sbuf(ctx, "in2", [P, 2, P])
    span = sbuf(ctx, "span", [P, 2])
    row = sbuf(ctx, "visit_row", [1, 2 * P])
    cnt = sbuf(ctx, "visit_cnt", [1, P])
    cnt_i = sbuf(ctx, "visit_cnt_i", [1, P], I32)
    tot = sbuf(ctx, "visit_tot", [1, 4])
    tot_i = sbuf(ctx, "visit_tot_i", [1, 2], I32)
    ends_d = nc.dram_tensor("tile_ends", (2, RB * P), FP32, kind="Internal").ap()
    ps = psum(ctx, "ps_p")

    def s_(name):
        return sem(ctx, "p_" + name)
    padded, loaded, consts, floats, turned = map(s_, ("padded", "loaded", "consts", "floats", "turned"))
    reduced, written, spread, dve, tiles_ok = map(s_, ("reduced", "written", "spread", "dve", "tiles_ok"))
    listed, span_ok = map(s_, ("listed", "span_ok"))
    fetched = [sem(ctx, f"p_fetched{i}", pool_dma=True) for i in range(2)]
    full = RB * P * P

    with nc.Block() as block:
        @block.gpsimd
        def _(gp):
            gp.memset(raw["src"][:, RB - 1, :], 0).then_inc(padded, 1)
            gp.memset(raw["dst"][:, RB - 1, :], NOWHERE).then_inc(padded, 1)
            gp.memset(pad["src"][:, :], 0).then_inc(padded, 1)
            gp.memset(pad["dst"][:, :], NOWHERE).then_inc(padded, 1)
            gp.iota(iota_i[:, :], [[1, RB * P]], base=0, channel_multiplier=0).then_inc(consts, 1)
            gp.iota(node0_i[:, :], [[P - 1, 2]], base=0, channel_multiplier=P).then_inc(consts, 1)
            gp.memset(k["ident"][:, :], 0.0).then_inc(consts, 1)
            gp.wait_ge(consts, 3)
            gp.affine_select(out=k["ident"][:, :], in_=k["ident"][:, :], compare_op=ALU.not_equal, fill=1.0,
                             base=0, pattern=[[-1, P]], channel_multiplier=1).then_inc(consts, 1)
            gp.memset(k["zeros"][:, :], 0.0).then_inc(consts, 1)
            gp.memset(k["node"][:, :, 2 * H:ND], 1.0).then_inc(consts, 1)
            gp.memset(k["zmax"][:, :], -HUGE).then_inc(consts, 1)
            gp.memset(k["amax"][:, :], -HUGE).then_inc(consts, 1)
            gp.wait_ge(listed, 64)
            gp.wait_ge(tiles_ok, 1)
            for i in range(2):
                gp.indirect_dma_start(out=edge_i[:, i, :], out_offset=None,
                                      in_=scratch["dst_p"].rearrange("(r c) -> r c", c=P),
                                      in_offset=bass.IndirectOffsetOnAxis(ap=tiles_i[:, i:i + 1], axis=0)).then_inc(fetched[i], 16)

        @block.sync
        def _(sp):
            sp.wait_ge(padded, 4)
            r = ET - 1 - (RB - 1) * P
            for name in ("dst", "src"):
                e = a[name]
                sp.dma_start(raw[name][:, 0:RB - 1, :],
                             e[0:(RB - 1) * P * P].rearrange("(b r c) -> r b c", r=P, c=P)).then_inc(loaded, 16)
                sp.dma_start(raw[name][0:r, RB - 1, :],
                             e[(RB - 1) * P * P:(ET - 1) * P].rearrange("(r c) -> r c", c=P)).then_inc(loaded, 16)
                sp.dma_start(raw[name][r:r + 1, RB - 1, 0:ETAIL],
                             e[(ET - 1) * P:E].rearrange("(r c) -> r c", r=1)).then_inc(loaded, 16)
            sp.wait_ge(loaded, 96)
            for name in ("dst", "src"):
                to = scratch[name + "_p"]
                sp.dma_start(to[0:full].rearrange("(b r c) -> r b c", r=P, c=P), raw[name][:, :, :]).then_inc(listed, 16)
                sp.dma_start(to[full:EROWS * P].rearrange("(r c) -> r c", c=P), pad[name][:, :]).then_inc(listed, 16)
            sp.wait_ge(reduced, 2)
            for i in range(2):
                with nc.allow_non_contiguous_dma(reason="one value an edge tile"):
                    sp.dma_start(ends_d[i, :].rearrange("(b r) -> r b", r=P), ends[:, i, :]).then_inc(written, 16)
            sp.wait_ge(written, 32)
            for i, to in enumerate((lows, highs)):
                sp.dma_start(to[:, :], ends_d[i:i + 1, :].to_broadcast([P, RB * P])).then_inc(spread, 16)
            sp.wait_ge(listed, 64)

        @block.vector
        def _(v):
            n = [0]

            def step(ins):
                n[0] += 1
                ins.then_inc(dve, 1)
                v.wait_ge(dve, n[0])
            v.wait_ge(loaded, 96)
            nc.vector.tensor_copy(dst_f[:, :, :], raw["dst"][:, :, :]).then_inc(floats, 1)
            v.wait_ge(floats, 1)
            nc.vector.tensor_reduce(ends[:, 0, :], dst_f[:, :, :], AX.X, MIN).then_inc(reduced, 1)
            nc.vector.tensor_reduce(ends[:, 1, :], dst_f[:, :, :], AX.X, MAX).then_inc(reduced, 1)
            v.wait_ge(consts, 8)
            step(nc.vector.tensor_copy(tile_no[:, :], iota_i[:, :]))
            step(nc.vector.tensor_copy(k["iota"][:, :], iota_i[:, 0:P]))
            step(nc.vector.tensor_copy(node0[:, :], node0_i[:, :]))
            v.wait_ge(spread, 32)
            step(nc.vector.tensor_scalar(v1[:, :], lows[:, :], node0[:, 1:2], None, ALU.is_le))
            step(nc.vector.tensor_scalar(v2[:, :], highs[:, :], node0[:, 0:1], None, ALU.is_ge))
            step(nc.vector.tensor_tensor(v1[:, :], v1[:, :], v2[:, :], MUL))
            step(nc.vector.scalar_tensor_tensor(v2[:, :], tile_no[:, :], -float(ET - 1), v1[:, :], ADD, MUL))
            step(nc.vector.tensor_tensor(lows[:, :], tile_no[:, :], v1[:, :], MUL))
            step(nc.vector.tensor_reduce(tiles[:, 0:1], v2[:, :], AX.X, MIN))
            step(nc.vector.tensor_scalar(tiles[:, 0:1], tiles[:, 0:1], float(ET - 1), None, ADD))
            step(nc.vector.tensor_reduce(tiles[:, 1:2], lows[:, :], AX.X, MAX))
            nc.vector.tensor_copy(tiles_i[:, :], tiles[:, :]).then_inc(tiles_ok, 1)
            for i in range(2):
                v.wait_ge(fetched[i], 16)
            step(nc.vector.tensor_copy(edge[:, :, :], edge_i[:, :, :]))
            step(nc.vector.tensor_scalar(in1[:, :, :], edge[:, :, :], node0[:, 1:2], None, ALU.is_le))
            step(nc.vector.tensor_scalar(in2[:, :, :], edge[:, :, :], node0[:, 0:1], None, ALU.is_ge))
            step(nc.vector.tensor_tensor(in1[:, :, :], in1[:, :, :], in2[:, :, :], MUL))
            step(nc.vector.scalar_tensor_tensor(in2[:, 0, :], k["iota"][:, :], -float(P), in1[:, 0, :], ADD, MUL))
            step(nc.vector.scalar_tensor_tensor(in2[:, 1, :], k["iota"][:, :], 1.0, in1[:, 1, :], ADD, MUL))
            step(nc.vector.tensor_reduce(span[:, 0:1], in2[:, 0, :], AX.X, MIN))
            step(nc.vector.tensor_reduce(span[:, 1:2], in2[:, 1, :], AX.X, MAX))
            step(nc.vector.tensor_scalar(span[:, 0:1], span[:, 0:1], float(P), None, ADD))
            nc.vector.scalar_tensor_tensor(span[:, :], tiles[:, :], float(P), span[:, :], MUL, ADD).then_inc(span_ok, 1)
            v.wait_ge(turned, 1)
            step(nc.vector.tensor_copy(row[:, :], ps[0:1, 0:2 * P]))
            step(nc.vector.tensor_tensor(cnt[:, :], row[:, P:2 * P], row[:, 0:P], SUB))
            step(nc.vector.tensor_copy(k["visits"][:, 0:P], row[:, 0:P]))
            step(nc.vector.tensor_scalar(cnt[:, :], cnt[:, :], 1.0 / CE, 0.5 - 0.5 / CE, MUL, ADD))
            step(nc.vector.tensor_scalar(cnt_i[:, :], cnt[:, :], float(MINC), None, MAX))
            step(nc.vector.tensor_copy(cnt[:, :], cnt_i[:, :]))
            step(nc.vector.tensor_reduce(tot[:, 0:1], cnt[:, 0:NT], AX.X, ADD))
            step(nc.vector.tensor_scalar(tot_i[:, 0:1], tot[:, 0:1], 1.0 / RING, 0.5 - 0.5 / RING, MUL, ADD))
            step(nc.vector.tensor_copy(tot[:, 1:2], tot_i[:, 0:1]))
            step(nc.vector.tensor_copy(k["visits"][:, 2 * VT:2 * VT + 1], tot_i[:, 0:1]))
            step(nc.vector.scalar_tensor_tensor(tot[:, 2:3], tot[:, 1:2], float(RING), tot[:, 0:1], MUL, SUB))
            step(nc.vector.tensor_tensor(cnt[:, NT - 1:NT], cnt[:, NT - 1:NT], tot[:, 2:3], ADD))
            step(nc.vector.tensor_copy(k["visits"][:, VT:VT + P], cnt[:, :]))

        @block.tensor
        def _(pe):
            pe.wait_ge(consts, 8)
            pe.wait_ge(span_ok, 1)
            nc.tensor.transpose(ps[0:1, 0:P], span[:, 0:1], k["ident"][:, :])
            nc.tensor.transpose(ps[0:1, P:2 * P], span[:, 1:2], k["ident"][:, :]).then_inc(turned, 1)


def project_attention(nc, a, k, scratch, ctx, sem, sbuf, psum):
    w = sbuf(ctx, "w_att", [P, KB, D + 2 * H])
    att = sbuf(ctx, "att_vec", [P, 2, D])
    tmp = sbuf(ctx, "w_tmp", [P, D])
    mhalf = sbuf(ctx, "mhalf1", [P, GT])
    xg = [sbuf(ctx, f"xg{i}", [P, GT, D]) for i in range(2)]
    xl = [sbuf(ctx, f"xl{i}", [P, GT, D]) for i in range(2)]
    hrow = [sbuf(ctx, f"hrow{i}", [P, GT, NA]) for i in range(2)]
    st = [sbuf(ctx, f"bn_st{i}", [P, GT, 6]) for i in range(2)]
    mv = [sbuf(ctx, f"bn_mv{i}", [P, GT, 2]) for i in range(2)]
    ve = [sbuf(ctx, f"bn_ve{i}", [P, GT]) for i in range(2)]
    rs = [sbuf(ctx, f"bn_rs{i}", [P, GT]) for i in range(2)]
    xT = [sbuf(ctx, f"xT1_{i}", [P, D]) for i in range(2)]
    gmax = [sbuf(ctx, f"gmax{i}", [P, H]) for i in range(2)]
    zb = sbuf(ctx, "shift_z", [P, NT, H])
    ps_t = [psum(ctx, f"ps1_t{i}") for i in range(2)]
    ps_h = [psum(ctx, f"ps1_h{i}") for i in range(2)]

    w_in = sem(ctx, "a_w_in")
    fold = sem(ctx, "a_fold")
    x_in = [sem(ctx, f"a_x_in{i}") for i in range(2)]
    x_free = [sem(ctx, f"a_x_free{i}") for i in range(2)]
    const = sem(ctx, "a_const")
    stats = sem(ctx, "a_stats")
    aggr = sem(ctx, "a_aggr")
    eps = sem(ctx, "a_eps")
    rstd = sem(ctx, "a_rstd")
    normed = sem(ctx, "a_normed")
    resid = sem(ctx, "a_resid")
    turned = sem(ctx, "a_turned")
    xT_ok = sem(ctx, "a_xT")
    prod = sem(ctx, "a_prod")
    h_ok = sem(ctx, "a_h_ok")
    max_ok = sem(ctx, "a_max")
    r_out = [sem(ctx, f"a_r_out{i}") for i in range(2)]
    h_out = [sem(ctx, f"a_h_out{i}") for i in range(2)]
    mall = sem(ctx, "a_mall")
    shift = sem(ctx, "a_shift")
    passed = sem(ctx, "a_passed")

    def groups(eng, body):
        with eng.Fori(0, NG // 2 - 1) as i:
            for par in range(2):
                body(i * 2 + par, i, par, False)
        for par in range(2):
            body(NG - 2 + par, NG // 2 - 1, par, par == 1)

    def rows(dram, g, n=GT):
        return dram[bass.ds(g * (GT * P), n * P), :].rearrange("(t p) f -> p t f", p=P)

    with nc.Block() as block:
        @block.sync
        def _(sp):
            for b in range(KB):
                sp.dma_start(w[:, b, 0:D].rearrange("i (h o) -> i h o", h=H),
                             a["L0_gnn_W"][:, b * P:(b + 1) * P, :].rearrange("h i o -> i h o")).then_inc(w_in, 16)
            for i, name in enumerate(("L0_gnn_a_src", "L0_gnn_a_dst")):
                sp.dma_start(att[:, i, :], a[name].rearrange("h o x -> x (h o)").to_broadcast([P, D])).then_inc(w_in, 16)

            def load(g, i, par, last):
                sp.wait_ge(x_free[par], i * 16 + 16)
                if not last:
                    sp.dma_start(xg[par][:, :, :], rows(a["x"], g)).then_inc(x_in[par], 16)
                else:
                    sp.dma_start(xg[par][:, 0:GT - 1, :], rows(a["x"], g, GT - 1)).then_inc(x_in[par], 16)
                    sp.wait_ge(x_in[par], 16 * (i + 1))
                    sp.dma_start(xg[par][0:TAIL, GT - 1, :], a["x"][(NT - 1) * P:N, :]).then_inc(x_in[par], 16)
            groups(sp, load)

        @block.vector
        def _(v):
            v.wait_ge(w_in, 64)
            n = 0
            for b in range(KB):
                for i in range(2):
                    nc.vector.tensor_tensor(tmp[:, :], w[:, b, 0:D], att[:, i, :], MUL).then_inc(fold, 1)
                    v.wait_ge(fold, n + 1)
                    nc.vector.tensor_reduce(w[:, b, D + i * H:D + (i + 1) * H],
                                            tmp[:, :].rearrange("p (h o) -> p h o", h=H), AX.X, ADD).then_inc(fold, 1)
                    v.wait_ge(fold, n + 2)
                    n += 2

            def body(g, i, par, last):
                v.wait_ge(x_in[par], i * 16 + (32 if last else 16))
                for j in range(GT):
                    nc.vector.bn_stats(st[par][:, j, :], xg[par][:, j, :]).then_inc(stats, 1)
                v.wait_ge(stats, g * GT + GT)
                hold(v, passed)
                for j in range(GT):
                    nc.vector.bn_aggr(mv[par][:, j, :], st[par][:, j, :]).then_inc(aggr, 1)
                v.wait_ge(rstd, g + 1)
                for j in range(GT):
                    nc.vector.tensor_scalar(xl[par][:, j, :], xg[par][:, j, :], mv[par][:, j, 0:1],
                                            rs[par][:, j:j + 1], SUB, MUL).then_inc(normed, 1)
                v.wait_ge(normed, g * GT + GT)
                nc.vector.tensor_tensor(xg[par][:, :, :], xg[par][:, :, :], xl[par][:, :, :], ADD).then_inc(resid, 1)
                v.wait_ge(h_ok, g * GT + GT)
                nc.vector.tensor_reduce(gmax[par][:, :], hrow[par][:, :, D:NA].rearrange("p t h -> p h t"), AX.X, MAX)\
                    .then_inc(max_ok, 1)
                v.wait_ge(max_ok, g * 2 + 1)
                nc.vector.tensor_tensor(k["amax"][:, :], k["amax"][:, :], gmax[par][:, :], MAX).then_inc(max_ok, 1)

            groups(v, body)
            v.wait_ge(mall, 1)
            nc.vector.tensor_tensor(zb[:, :, :], k["node"][:, :, 0:H],
                                    k["amax"][:, :].rearrange("p (x h) -> p x h", x=1).to_broadcast([P, NT, H]), ADD)\
                .then_inc(shift, 1)
            v.wait_ge(shift, 1)
            nc.vector.scalar_tensor_tensor(k["node"][:, :, H:2 * H], zb[:, :, :], LEAK, zb[:, :, :], MUL, MAX)\
                .then_inc(shift, 1)

        @block.gpsimd
        def _(gp):
            gp.memset(mhalf[:, :], -0.5).then_inc(const, 1)
            gp.wait_ge(const, 1)

            def body(g, i, par, last):
                gp.wait_ge(aggr, g * GT + GT)
                hold(gp, passed)
                gp.tensor_scalar(ve[par][:, :], mv[par][:, :, 1], LN_EPS, None, ADD).then_inc(eps, 1)
                gp.wait_ge(eps, g + 1)
                gp.tensor_tensor(rs[par][:, :], ve[par][:, :], mhalf[:, :], ALU.pow).then_inc(rstd, 1)
            groups(gp, body)
            gp.wait_ge(max_ok, 2 * NG)
            gp.partition_all_reduce(k["amax"][:, :], k["amax"][:, :], P, REDUCE_MAX).then_inc(mall, 1)

        @block.tensor
        def _(pe):
            pe.wait_ge(fold, 4 * KB)

            def body(g, i, par, last):
                pe.wait_ge(normed, g * GT + GT)
                for j in range(GT + 1):
                    if j < GT:
                        t = g * GT + j
                        b = j % 2
                        if j >= 2:
                            pe.wait_ge(xT_ok, t - 1)
                        for q in range(KB):
                            last_i = nc.tensor.transpose(ps_t[b][:, q * P:(q + 1) * P], xl[par][:, j, q * P:(q + 1) * P],
                                                         k["ident"][:, :])
                        last_i.then_inc(turned, 1)
                    if j:
                        t = g * GT + j - 1
                        b = (j - 1) % 2
                        pe.wait_ge(xT_ok, t + 1)
                        if j > 2:
                            pe.wait_ge(h_ok, t - 1)
                        for q in range(KB):
                            last_i = nc.tensor.matmul(ps_h[b][:, 0:D + 2 * H], xT[b][:, q * P:(q + 1) * P], w[:, q, :],
                                                      start=q == 0, stop=q == KB - 1)
                        last_i.then_inc(prod, 1)
                pe.wait_ge(h_ok, g * GT + GT)
            groups(pe, body)

        @block.scalar
        def _(s):
            for par in range(2):
                first_turn(s, k, x_free[par])
                first_turn(s, k, h_out[par])

            def body(g, i, par, last):
                s.wait_ge(h_out[par], i * 16 + 16)
                for j in range(GT + 1):
                    if j < GT:
                        t = g * GT + j
                        b = j % 2
                        s.wait_ge(turned, t + 1)
                        nc.scalar.copy(xT[b][:, :], ps_t[b][:, 0:D]).then_inc(xT_ok, 1)
                    if j:
                        t = g * GT + j - 1
                        b = (j - 1) % 2
                        s.wait_ge(prod, t + 1)
                        nc.scalar.copy(hrow[par][:, j - 1, :], ps_h[b][:, 0:NA])
                        nc.scalar.copy(k["node"][:, bass.ds(t, 1), 0:H].rearrange("p x h -> p (x h)"),
                                       ps_h[b][:, NA:NA + H]).then_inc(h_ok, 1)
                s.wait_ge(h_ok, g * GT + GT)
                s.dma_start(rows(scratch["tab_a"], g), hrow[par][:, :, :]).then_inc(h_out[par], 16)
                s.wait_ge(resid, g + 1)
                s.dma_start(rows(scratch["resid_a"], g), xg[par][:, :, :]).then_inc(x_free[par], 16)
            groups(s, body)
            for par in range(2):
                s.wait_ge(h_out[par], 16 * (NG // 2 + 1))
                s.wait_ge(x_free[par], 16 * (NG // 2 + 1))


def hold(eng, passed):
    eng.sem_inc(passed, 1)


class Gather:
    def __init__(self, nc, k, scratch, table, width, tag, ctx, sem, sbuf):
        self.nc, self.k, self.scratch, self.table, self.tag = nc, k, scratch, table, tag
        self.rows = sbuf(ctx, f"{tag}_ring", [P, RING * CH, width])
        self.src = sbuf(ctx, f"{tag}_src", [P, RING, CH], I32)
        self.dst = sbuf(ctx, f"{tag}_dst", [P, RING, CH], I32)
        self.staged = sem(ctx, f"{tag}_staged")
        self.gathered = [sem(ctx, f"{tag}_gathered{c}", pool_dma=True) for c in range(RING)]
        self.ready = sem(ctx, f"{tag}_ready")
        self.free = sem(ctx, f"{tag}_free")
        self.passed = sem(ctx, f"{tag}_passed")

    def stage(self, sp):
        k, g_ = self.k, self

        def chunk(g, e0):
            sp.wait_ge(g_.free, g + 1)
            for to, name in ((g_.src, "src_p"), (g_.dst, "dst_p")):
                sp.dma_start(to[:, bass.ds(g % RING, 1), :].rearrange("p x c -> p (x c)"),
                             g_.scratch[name][bass.ds(e0, CE)].rearrange("(p c) -> p c", c=CH)).then_inc(g_.staged, 16)
            sp.wait_ge(g_.staged, g * 32 + 32)
        done = sp.alloc_register(f"{g_.tag}_sp_done")
        edge = sp.alloc_register(f"{g_.tag}_sp_edge")
        sp.reg_mov(done, 0)
        with sp.Fori(0, NT) as n:
            count = sp.value_load(k["visits"][0:1, bass.ds(n + VT, 1)], min_val=MINC, max_val=ET)
            sp.reg_mov(edge, sp.value_load(k["visits"][0:1, bass.ds(n, 1)], min_val=0, max_val=ET * P))
            with sp.Fori(0, count):
                chunk(sp.snap(done, min_val=0, max_val=NT * ET), sp.snap(edge, min_val=0, max_val=(EROWS - CH) * P))
                sp.reg_add(done, done, 1)
                sp.reg_add(edge, edge, CE)

    def gather(self, gp):
        k, g_ = self.k, self
        rounds = gp.value_load(k["visits"][0:1, 2 * VT:2 * VT + 1], min_val=2, max_val=NT * ET)

        def ring_round(r, first):
            for c in range(RING):
                gp.wait_ge(g_.staged, r * (32 * RING) + 32 * (c + 1))
                gp.wait_ge(g_.free, r * RING + (c + 1))
                hold(gp, g_.passed)
                for j in range(CH):
                    gp.indirect_dma_start(out=g_.rows[:, c * CH + j, :], out_offset=None, in_=g_.table,
                                          in_offset=bass.IndirectOffsetOnAxis(ap=g_.src[:, c, j:j + 1], axis=0))\
                        .then_inc(g_.gathered[c], 16)
                if c:
                    gp.wait_ge(g_.gathered[c - 1], r * (16 * CH) + 16 * CH)
                    gp.sem_inc(g_.ready, 1)
                elif not first:
                    gp.wait_ge(g_.gathered[RING - 1], r * (16 * CH))
                    gp.sem_inc(g_.ready, 1)
        ring_round(0, True)
        with gp.Fori(1, rounds) as r:
            ring_round(r, False)
        gp.wait_ge(g_.gathered[RING - 1], rounds * (16 * CH))
        gp.sem_inc(g_.ready, 1)

    def slot(self, g, j, n=1):
        return self.rows[:, bass.ds((g % RING) * CH + j, n), :]


def node_tiles(eng, k, name, start, first_chunk, chunk, end):
    done = eng.alloc_register(name)
    eng.reg_mov(done, 0)

    def tile(n, par, half):
        count = eng.value_load(k["visits"][0:1, bass.ds(n + VT, 1)], min_val=MINC, max_val=ET)
        start(n, par)
        first_chunk(0 if half is None else eng.snap(done, min_val=1, max_val=NT * ET), n, par, half)
        eng.reg_add(done, done, 1)
        with eng.Fori(1, count):
            chunk(eng.snap(done, min_val=1, max_val=NT * ET), n, par)
            eng.reg_add(done, done, 1)
    tile(0, 0, None)
    with eng.Fori(0, NT // 2 - 1) as i:
        tile(i * 2 + 1, 1, i)
        tile(i * 2 + 2, 0, i)
    tile(NT - 1, 1, NT // 2 - 1)
    end(eng.snap(done, min_val=1, max_val=NT * ET), 1)


def node_numbers(nc, k, v, node_no, nodes_ok, passed):
    for par in range(2):
        nc.vector.tensor_scalar(node_no[par][:, :], k["iota"][:, :], float((par - 2) * P), None, ADD).then_inc(nodes_ok, 1)

    def start(n, par):
        v.wait_ge(nodes_ok, n + 1)
        nc.vector.tensor_scalar(node_no[par][:, :], node_no[par][:, :], float(2 * P), None, ADD).then_inc(nodes_ok, 1)
        v.wait_ge(nodes_ok, n + 3)
        hold(v, passed)
    return start


def incidence(nc, v, gat, to, node_no, g, b, par):
    return nc.vector.tensor_tensor(
        to,
        node_no[par][:, :].rearrange("p (x n) -> p x n", x=1).to_broadcast([P, HT, P]),
        gat.dst[:, bass.ds(g % RING, 1), b * HT:(b + 1) * HT].rearrange("p x (t y) -> p (x t) y", y=1)
        .to_broadcast([P, HT, P]),
        ALU.is_equal)


def nothing(*args):
    pass


class Split:
    def __init__(self, sbuf, ctx, name, shape):
        self.high = sbuf(ctx, name + "_high", shape, F32R)
        self.low = sbuf(ctx, name + "_low", shape, F32R)

    def lower(self, nc, full, *index):
        high, low = self.at(*index)
        return nc.vector.tensor_tensor(low, full, high.bitcast(FP32), SUB)

    def at(self, *index):
        index = (slice(None),) + index
        return self.high[index], self.low[index]


def products_of(nc, out, pairs):
    steps = [(x, y, i, j) for i, j in ((0, 1), (1, 0), (0, 0)) for x, y in pairs]
    for n, (x, y, i, j) in enumerate(steps):
        last = nc.tensor.matmul(out, x[i], y[j], start=n == 0, stop=n == len(steps) - 1)
    return last


def attention_edges(nc, k, scratch, ctx, sem, sbuf, psum):
    tag = "ea"
    gat = Gather(nc, k, scratch, scratch["tab_a"], NA, tag, ctx, sem, sbuf)
    node_no = [sbuf(ctx, f"ea_nodes{i}", [P, P]) for i in range(2)]
    S1 = sbuf(ctx, "ea_S1", [P, 2 * CH, P], BF16)
    ident = sbuf(ctx, "ea_ident", [P, P], BF16)
    w = sbuf(ctx, "ea_w", [P, CH, H])
    NR = ND + 1
    rows = sbuf(ctx, "ea_rows", [P, NT, NR])
    node = sbuf(ctx, "ea_node", [P, NT, 2, NR], F32R)
    e = sbuf(ctx, "ea_e_sum", [P, CH, ND])
    S2 = sbuf(ctx, "ea_S2", [P, CH, P])
    ST = sbuf(ctx, "ea_ST", [P, CH, P], F32R)
    V = sbuf(ctx, "ea_V", [P, CH, NV])
    z = sbuf(ctx, "ea_z", [P, CH, H])
    mk = sbuf(ctx, "ea_mk", [P, CH])
    lk = sbuf(ctx, "ea_lk", [P, CH, H])
    res = [sbuf(ctx, f"ea_res{i}", [P, NV]) for i in range(2)]
    ps_acc = [psum(ctx, f"ea_acc{i}") for i in range(2)]
    ps_t = [psum(ctx, f"ea_t{i}") for i in range(2)]
    ps_e = psum(ctx, "ea_e")

    def s_(name):
        return sem(ctx, "ea_" + name)
    nodes_ok, S1_ok, T_ok, ST_ok, S2_ok, E_ok, summed = map(s_, ("nodes", "S1_ok", "T_ok", "ST_ok", "S2_ok", "E_ok", "summed"))
    z_ok, mk_ok, zm_ok, lk_ok, max_ok, dl_ok, w_ok, V_ok = map(s_, (
        "z_ok", "mk_ok", "zm_ok", "lk_ok", "max_ok", "dl_ok", "w_ok", "V_ok"))
    ones_ok, acc_ok, acc_free, wV_ok = map(s_, ("ones", "acc_ok", "acc_free", "wV_ok"))
    rows_ok, high_ok, low_ok, e_ok = map(s_, ("rows_ok", "high_ok", "low_ok", "e_ok"))
    res_out = [sem(ctx, f"ea_res_out{i}") for i in range(2)]

    def half_of(g, b):
        return S1[:, bass.ds((g % 2) * CH + b * HT, HT), :]

    with nc.Block() as block:
        @block.sync
        def _(sp):
            gat.stage(sp)

        @block.gpsimd
        def _(gp):
            gat.gather(gp)

        @block.vector
        def _(v):
            v.sem_inc(gat.free, RING)
            v.sem_inc(V_ok, 2)
            nc.vector.memset(V[:, :, NA:NV], 1.0).then_inc(ones_ok, 1)
            nc.vector.tensor_copy(ident[:, :], k["ident"][:, :]).then_inc(ones_ok, 1)
            nc.vector.memset(rows[:, :, ND:NR], 0.0).then_inc(rows_ok, 1)
            nc.vector.tensor_copy(rows[:, :, 0:ND], k["node"][:, :, :]).then_inc(rows_ok, 1)
            v.wait_ge(rows_ok, 2)
            v.wait_ge(high_ok, 1)
            nc.vector.tensor_tensor(node[:, :, 1, :], rows[:, :, :], node[:, :, 0, :].bitcast(FP32), SUB).then_inc(low_ok, 1)
            start = node_numbers(nc, k, v, node_no, nodes_ok, gat.passed)

            def build(g, n, par):
                v.wait_ge(gat.staged, g * 32 + 32)
                for b in range(2):
                    v.wait_ge(S2_ok, g * 2 + (b + 1))
                    incidence(nc, v, gat, half_of(g, b), node_no, g, b, par).then_inc(S1_ok, 1)

            def weigh(g):
                v.wait_ge(w_ok, g)
                for b in range(2):
                    v.wait_ge(summed, g * 2 + (b + 1))
                    nc.vector.tensor_tensor(
                        V[:, b * HT:(b + 1) * HT, 0:D].rearrange("p t (h o) -> p t h o", h=H),
                        gat.slot(g - 1, b * HT, HT)[:, :, 0:D].rearrange("p t (h o) -> p t h o", h=H),
                        w[:, b * HT:(b + 1) * HT, :].rearrange("p t (h x) -> p t h x", x=1).to_broadcast([P, HT, H, HD]),
                        MUL).then_inc(V_ok, 1)

            def scores(g):
                v.wait_ge(gat.ready, g + 1)
                v.wait_ge(E_ok, g + 1)
                parts = ps_e[:, 0:CH * 64].rearrange("p (t c) -> p t c", t=CH)[:, :, 0:2 * NR]
                nc.vector.tensor_reduce(e[:, :, :], parts.rearrange("p t (y c) -> p t c y", y=2)[:, :, 0:ND, :], AX.X, ADD)\
                    .then_inc(e_ok, 1)
                v.wait_ge(e_ok, g + 1)
                nc.vector.tensor_tensor(z[:, :, :], e[:, :, 0:H], gat.slot(g, 0, CH)[:, :, D:NA], ADD).then_inc(z_ok, 1)
                nc.vector.tensor_scalar(mk[:, :], e[:, :, 2 * H], HUGE, -HUGE, MUL, ADD).then_inc(mk_ok, 1)
                v.wait_ge(z_ok, g + 1)
                v.wait_ge(mk_ok, g + 1)
                nc.vector.tensor_tensor(z[:, :, :], z[:, :, :],
                                        mk[:, :].rearrange("p (t x) -> p t x", x=1).to_broadcast([P, CH, H]), ADD)\
                    .then_inc(zm_ok, 1)
                v.wait_ge(zm_ok, g + 1)
                nc.vector.scalar_tensor_tensor(lk[:, :, :], z[:, :, :], LEAK, z[:, :, :], MUL, MAX).then_inc(lk_ok, 1)
                nc.vector.tensor_tensor(k["zmax"][:, :], k["zmax"][:, :],
                                        z[:, :, :].rearrange("p t h -> p (t h)"), MAX).then_inc(max_ok, 1)
                v.wait_ge(lk_ok, g + 1)
                nc.vector.tensor_tensor(lk[:, :, :], lk[:, :, :], e[:, :, H:2 * H], SUB).then_inc(dl_ok, 1)
                v.wait_ge(max_ok, g + 1)

            def release(g):
                v.wait_ge(V_ok, g * 2 + 2)
                v.sem_inc(gat.free, 1)

            def first_chunk(g, n, par, half):
                build(g, n, par)
                if half is not None:
                    weigh(g)
                scores(g)
                if half is not None:
                    release(g)

            def chunk(g, n, par):
                build(g, n, par)
                weigh(g)
                scores(g)
                release(g)

            def end(g, par):
                weigh(g)
                release(g)
            node_tiles(v, k, "ea_dve", start, first_chunk, chunk, end)

        @block.tensor
        def _(pe):
            pe.wait_ge(ones_ok, 2)
            pe.wait_ge(low_ok, 1)
            pe.sem_inc(summed, 4)

            def turn(g):
                for b in range(2):
                    pe.wait_ge(S1_ok, g * 2 + (b + 1))
                    hold(pe, gat.passed)
                    for j in range(HT):
                        last = nc.tensor.matmul(ps_t[b][:, j * P:(j + 1) * P],
                                                half_of(g, b)[:, j:j + 1, :].rearrange("p x n -> p (x n)"), ident[:, :],
                                                start=True, stop=True)
                    last.then_inc(T_ok, 1)

            def hand_out(g, n):
                pe.wait_ge(ST_ok, g * 2 + 2)
                for j in range(CH):
                    last = nc.tensor.matmul(ps_e[:, j * 64:j * 64 + 2 * NR], ST[:, j, :],
                                            node[:, bass.ds(n, 1), :, :].rearrange("p x y c -> p (x y c)"),
                                            start=True, stop=True)
                last.then_inc(E_ok, 1)

            def add_up(g, b, par):
                pe.wait_ge(S2_ok, g * 2 + (b + 3))
                pe.wait_ge(V_ok, g * 2 + (b + 1))
                pe.wait_ge(wV_ok, g)
                for j in range(b * HT, (b + 1) * HT):
                    last = nc.tensor.matmul(ps_acc[par][:, 0:NV], S2[:, j, :], V[:, j, :], start=False, stop=False)
                last.then_inc(summed, 1)

            def first_chunk(g, n, par, half):
                turn(g)
                if half is not None:
                    add_up(g, 0, 1 - par)
                hand_out(g, n)
                if half is not None:
                    add_up(g, 1, 1 - par)
                    close_sum(1 - par)
                pe.wait_ge(acc_free, n + 1)
                nc.tensor.matmul(ps_acc[par][:, 0:NV], k["zeros"][:, 0:P], k["zeros"][:, :], start=True, stop=False)

            def close_sum(par):
                nc.tensor.matmul(ps_acc[par][:, 0:NV], k["zeros"][:, 0:P], k["zeros"][:, :], start=False, stop=True)\
                    .then_inc(acc_ok, 1)

            def chunk(g, n, par):
                turn(g)
                add_up(g, 0, par)
                hand_out(g, n)
                add_up(g, 1, par)

            def end(g, par):
                for b in range(2):
                    add_up(g, b, par)
                close_sum(par)
            node_tiles(pe, k, "ea_pe", nothing, first_chunk, chunk, end)

        @block.scalar
        def _(s):
            s.sem_inc(acc_free, 2)
            s.wait_ge(rows_ok, 2)
            nc.scalar.copy(node[:, :, 0, :], rows[:, :, :]).then_inc(high_ok, 1)
            s.sem_inc(S2_ok, 4)
            for par in range(2):
                first_turn(s, k, res_out[par])

            def chunk(g, n, par):
                for b in range(2):
                    s.wait_ge(T_ok, g * 2 + (b + 1))
                    nc.scalar.copy(ST[:, b * HT:(b + 1) * HT, :].rearrange("p t n -> p (t n)"), ps_t[b][:, 0:HT * P])\
                        .then_inc(ST_ok, 1)
                s.wait_ge(dl_ok, g + 1)
                nc.scalar.activation(w[:, :, :], lk[:, :, :], ACT.Exp).then_inc(w_ok, 1)
                for b in range(2):
                    s.wait_ge(summed, g * 2 + (b + 3))
                    hold(s, gat.passed)
                    nc.scalar.copy(S2[:, b * HT:(b + 1) * HT, :], half_of(g, b)).then_inc(S2_ok, 1)
                s.wait_ge(w_ok, g + 1)
                nc.scalar.copy(V[:, :, D:NA], w[:, :, :]).then_inc(wV_ok, 1)

            def copy_out(n, half, par):
                s.wait_ge(acc_ok, n + 1)
                s.wait_ge(res_out[par], half * 16 + 16)
                hold(s, gat.passed)
                nc.scalar.copy(res[par][:, :], ps_acc[par][:, 0:NV]).then_inc(acc_free, 1)
                s.wait_ge(acc_free, n + 3)
                s.dma_start(scratch["agg_a"][bass.ds(n * P, P), :], res[par][:, :]).then_inc(res_out[par], 16)

            def first_chunk(g, n, par, half):
                chunk(g, n, par)
                if half is not None:
                    copy_out(n - 1, half, 1 - par)

            def end(g, par):
                copy_out(NT - 1, NT // 2 - 1, par)
            node_tiles(s, k, "ea_act", nothing, first_chunk, chunk, end)
            for par in range(2):
                s.wait_ge(res_out[par], 16 * (NT // 2 + 1))


def mean_edges(nc, k, scratch, ctx, sem, sbuf, psum):
    gat = Gather(nc, k, scratch, scratch["tab_b"], D, "eb", ctx, sem, sbuf)
    node_no = [sbuf(ctx, f"eb_nodes{i}", [P, P]) for i in range(2)]
    S = sbuf(ctx, "eb_S", [P, CH, P])
    res = [sbuf(ctx, f"eb_res{i}", [P, D]) for i in range(2)]
    ps_acc = [psum(ctx, f"eb_acc{i}") for i in range(2)]

    def s_(name):
        return sem(ctx, "eb_" + name)
    nodes_ok, S_ok, summed, acc_ok, acc_free = map(s_, ("nodes", "S_ok", "summed", "acc_ok", "acc_free"))
    res_out = [s_(f"res_out{i}") for i in range(2)]

    with nc.Block() as block:
        @block.sync
        def _(sp):
            gat.stage(sp)

        @block.gpsimd
        def _(gp):
            gat.gather(gp)

        @block.vector
        def _(v):
            start = node_numbers(nc, k, v, node_no, nodes_ok, gat.passed)

            def chunk(g, n, par):
                v.wait_ge(gat.staged, g * 32 + 32)
                for b in range(2):
                    v.wait_ge(summed, g * 2 + (b + 1))
                    incidence(nc, v, gat, S[:, b * HT:(b + 1) * HT, :], node_no, g, b, par).then_inc(S_ok, 1)

            def first_chunk(g, n, par, half):
                chunk(g, n, par)
            node_tiles(v, k, "eb_dve", start, first_chunk, chunk, nothing)

        @block.tensor
        def _(pe):
            pe.sem_inc(gat.free, RING)
            pe.sem_inc(summed, 2)

            def zero(par, start):
                return nc.tensor.matmul(ps_acc[par][:, 0:D], k["zeros"][:, 0:P], k["zeros"][:, 0:D],
                                        start=start, stop=not start)

            def chunk(g, n, par):
                pe.wait_ge(gat.ready, g + 1)
                for b in range(2):
                    pe.wait_ge(S_ok, g * 2 + (b + 1))
                    for j in range(b * HT, (b + 1) * HT):
                        last = nc.tensor.matmul(ps_acc[par][:, 0:D], S[:, j, :],
                                                gat.slot(g, j).rearrange("p x f -> p (x f)"), start=False, stop=False)
                    last.then_inc(summed, 1)
                pe.wait_ge(summed, g * 2 + 4)
                pe.sem_inc(gat.free, 1)

            def first_chunk(g, n, par, half):
                if half is not None:
                    zero(1 - par, False).then_inc(acc_ok, 1)
                pe.wait_ge(acc_free, n + 1)
                zero(par, True)
                chunk(g, n, par)

            def end(g, par):
                zero(par, False).then_inc(acc_ok, 1)
            node_tiles(pe, k, "eb_pe", nothing, first_chunk, chunk, end)

        @block.scalar
        def _(s):
            s.sem_inc(acc_free, 2)
            for par in range(2):
                first_turn(s, k, res_out[par])

            def copy_out(n, half, par):
                s.wait_ge(acc_ok, n + 1)
                s.wait_ge(res_out[par], half * 16 + 16)
                nc.scalar.copy(res[par][:, :], ps_acc[par][:, 0:D]).then_inc(acc_free, 1)
                s.wait_ge(acc_free, n + 3)
                s.dma_start(scratch["agg_b"][bass.ds(n * P, P), :], res[par][:, :]).then_inc(res_out[par], 16)
            with s.Fori(0, NT // 2) as i:
                for par in range(2):
                    copy_out(i * 2 + par, i, par)
            for par in range(2):
                s.wait_ge(res_out[par], 16 * (NT // 2 + 1))


class Group:
    def __init__(self, n, half, par):
        self.n, self.half, self.par = n, half, par

    def next(self):
        return Group(self.n + 1, self.half + self.par, 1 - self.par)

    def prev(self):
        return Group(self.n - 1, self.half - 1 + self.par, 1 - self.par)


def mixture(nc, a, k, scratch, ctx, sem, sbuf, psum):
    Q = NT // GM
    assert Q * GM == NT and Q % 2 == 1
    T2 = GM * P
    W1, W2, Wo = (Split(sbuf, ctx, f"m{n}", [P, NX, KB, D]) for n in ("W1", "W2", "Wo"))
    Wr = sbuf(ctx, "mWr", [P, KB, NX])
    Wg = Split(sbuf, ctx, "mWg", [P, KB, 2 * D])
    bo = sbuf(ctx, "mbo", [NX, D])
    br = sbuf(ctx, "mbr", [P, NX])
    NB = NX * KB
    bn_rows = [sbuf(ctx, f"bn_rows{i}", [5 * NB, P]) for i in range(2)]
    bn_cols = [sbuf(ctx, f"bn_cols{i}", [P, 5, NB]) for i in range(2)]
    bn_s = [sbuf(ctx, f"bn_s{i}", [P, NB]) for i in range(2)]
    bn_b = [sbuf(ctx, f"bn_b{i}", [P, NB]) for i in range(2)]
    bn_v = [sbuf(ctx, f"bn_v{i}", [P, NB]) for i in range(2)]
    mhalf = sbuf(ctx, "mhalf3", [P, NB])
    zm = sbuf(ctx, "zm", [P, 3])
    fill = sbuf(ctx, "fill", [P, XW])
    corr = sbuf(ctx, "corr", [P, NT, H])
    pair = range(2)
    U = [sbuf(ctx, f"mU{i}", [P, GM, NV]) for i in pair]
    R = [sbuf(ctx, f"mR{i}", [P, GM, D]) for i in pair]
    den = [sbuf(ctx, f"mden{i}", [P, GM, H]) for i in pair]
    XL = sbuf(ctx, "mXL", [P, GM, D])
    XL2 = sbuf(ctx, "mXM", [P, GM, D])
    XF, XF2 = (sbuf(ctx, f"m{n}_full", [P, KB, T2]) for n in ("XT", "XU"))
    hf1, hf2 = ([sbuf(ctx, f"m{n}_full{i}", [P, KB, T2]) for i in pair] for n in ("h1", "h2"))
    XT = [Split(sbuf, ctx, f"mXT{i}", [P, KB, T2]) for i in pair]
    XT2 = Split(sbuf, ctx, "mXU", [P, KB, T2])
    acc = [sbuf(ctx, f"macc{i}", [P, GM, D]) for i in pair]
    PB = [sbuf(ctx, f"mPB{i}", [P, GM, 2 * D]) for i in pair]
    lg = [sbuf(ctx, f"mlg{i}", [P, GM, NX]) for i in pair]
    lm = [sbuf(ctx, f"mlm{i}", [P, GM]) for i in pair]
    ls = [sbuf(ctx, f"mls{i}", [P, GM]) for i in pair]
    wg = [sbuf(ctx, f"mwg{i}", [P, GM, NX]) for i in pair]
    wT = [sbuf(ctx, f"mwT{i}", [NX, GM, P]) for i in pair]
    st = [sbuf(ctx, f"mst{i}", [P, GM, 6]) for i in pair]
    mv = [sbuf(ctx, f"mmv{i}", [P, GM, 2]) for i in pair]
    ve = [sbuf(ctx, f"mve{i}", [P, GM]) for i in pair]
    rs = [sbuf(ctx, f"mrs{i}", [P, GM]) for i in pair]
    h1 = [Split(sbuf, ctx, f"mh1{i}", [P, KB, T2]) for i in pair]
    h2 = [Split(sbuf, ctx, f"mh2{i}", [P, KB, T2]) for i in pair]
    ps1 = [psum(ctx, f"m_ps1{i}") for i in pair]
    ps2 = [psum(ctx, f"m_ps2{i}") for i in pair]
    psY = [psum(ctx, f"m_psY{i}") for i in pair]
    psT = psum(ctx, "m_psT")
    psR = psum(ctx, "m_psR")

    def s_(name):
        return sem(ctx, "m_" + name)
    w_in, bn_in, bn_T, bn_copied, bn_eps, bn_pow, bn_sub, bn_ok = map(s_, (
        "w_in", "bn_in", "bn_T", "bn_copied", "bn_eps", "bn_pow", "bn_sub", "bn_ok"))
    const, zred, zall, zlk, cdiff, cexp, corr_ok = map(s_, ("const", "zred", "zall", "zlk", "cdiff", "cexp", "corr_ok"))
    g_in = [s_(f"g_in{i}") for i in pair]
    g_free, den_ok, rec_ok, att_ok, x1_ok = map(s_, ("g_free", "den_ok", "rec_ok", "att_ok", "x1_ok"))
    st_ok, mv_ok, ve_ok, rs_ok, xl_ok = map(s_, ("st_ok", "mv_ok", "ve_ok", "rs_ok", "xl_ok"))
    T_ok, XT_ok, lg_ps, lg_ok, lm_ok, ls_in, le_ok, ls_ok, lr_ok, wg_ok = map(s_, (
        "T_ok", "XT_ok", "lg_ps", "lg_ok", "lm_ok", "ls_in", "le_ok", "ls_ok", "lr_ok", "wg_ok"))
    wT_ps, wT_ok, bo_ps, acc_ok = map(s_, ("wT_ps", "wT_ok", "bo_ps", "acc_ok"))
    p1_ok, h1_ok, p2_ok, h2_ok, y_ps, y_ok = map(s_, ("p1_ok", "h1_ok", "p2_ok", "h2_ok", "y_ps", "y_ok"))
    T2_ok, XT2_ok, pr_ps, pr_ok = map(s_, ("T2_ok", "XT2_ok", "pr_ps", "pr_ok"))
    x2_out = [s_(f"x2_out{i}") for i in pair]
    passed, filled, fill_ok = map(s_, ("passed", "filled", "fill_ok"))
    h1_high = s_("h1_high")
    W_stage = [s_(f"W_stage{i}") for i in pair]
    W_high, W_low, XT_low, XT2_low, h1_low, h2_low = map(s_, ("W_high", "W_low", "XT_low", "XT2_low", "h1_low", "h2_low"))

    def groups(eng, body):
        body(Group(0, 0, 0), False, True)
        with eng.Fori(0, (Q - 3) // 2) as i:
            body(Group(i * 2 + 1, i, 1), True, True)
            body(Group(i * 2 + 2, i + 1, 0), True, True)
        body(Group(Q - 2, (Q - 3) // 2, 1), True, True)
        body(Group(Q - 1, (Q - 1) // 2, 0), True, False)

    stages = [(W, name, e) for W, name in ((W1, "W1"), (W2, "W2"), (Wo, "Wo")) for e in range(0, NX, 2)] + [(Wg, None, 0)]

    def staged(n):
        full = PB[n % 2]
        return full[:, :, :].rearrange("p e (k f) -> p e k f", k=KB) if stages[n][1] else full[:, :, :]

    def stage_part(n):
        W, name, e = stages[n]
        return (slice(e, e + 2),) if name else ()

    def rows(dram, q):
        return dram[bass.ds(q.n * T2, T2), :].rearrange("(t p) f -> p t f", p=P)

    with nc.Block() as block:
        @block.sync
        def _(sp):
            for i, names in enumerate((("b1", "g1", "be1", "m1", "v1"), ("b2", "g2", "be2", "m2", "v2"))):
                for j, name in enumerate(names):
                    sp.dma_start(bn_rows[i][j * NB:(j + 1) * NB, :],
                                 a["L0_ffn_" + name].rearrange("e (k p) -> (e k) p", p=P)).then_inc(bn_in, 16)

            def load(q):
                sp.wait_ge(g_free, q.n + 1)
                sp.dma_start(U[q.par][:, :, :], rows(scratch["agg_a"], q)).then_inc(g_in[q.par], 16)
                sp.dma_start(R[q.par][:, :, :], rows(scratch["resid_a"], q)).then_inc(g_in[q.par], 16)
            load(Group(0, 0, 0))
            for i in pair:
                first_turn(sp, k, x2_out[i], 3)
            sp.dma_start(Wr[:, :, :], a["L0_ffn_Wr"].rearrange("(k p) e -> p k e", p=P)).then_inc(w_in, 16)
            sp.dma_start(br[:, :], a["L0_ffn_br"].rearrange("(x e) -> x e", x=1).to_broadcast([P, NX])).then_inc(w_in, 16)
            sp.dma_start(bo[:, :], a["L0_ffn_bo"]).then_inc(w_in, 16)
            for n, (W, name, e) in enumerate(stages):
                if n >= 2:
                    sp.wait_ge(W_low, n - 1)
                if name:
                    for j in range(2):
                        sp.dma_start(staged(n)[:, j, :, :], a["L0_ffn_" + name][e + j, :, :].rearrange("(k p) f -> p k f", p=P))\
                            .then_inc(W_stage[n % 2], 16)
                else:
                    for j in range(2):
                        sp.dma_start(PB[n % 2][:, :, j * D:(j + 1) * D],
                                     a["L1_gnn_weight"][j * D:(j + 1) * D, :].rearrange("(k p) f -> p k f", p=P))\
                            .then_inc(W_stage[n % 2], 16)
            load(Group(1, 0, 1))

            def body(q, before, after):
                if after and not (isinstance(q.n, int) and q.n + 2 >= Q):
                    load(q.next().next())
                sp.dma_start(scratch["buf"][bass.ds(q.n * (FILL * P), FILL * P), :].rearrange("(t p) f -> p t f", p=P),
                             fill[:, :].rearrange("p (x f) -> p x f", x=1).to_broadcast([P, FILL, XW])).then_inc(filled, 16)
                sp.wait_ge(pr_ok, q.n * GM + GM)
                sp.dma_start(rows(scratch["x2"], q), acc[q.par][:, :, :]).then_inc(x2_out[q.par], 16)
                sp.dma_start(rows(scratch["top_b"], q), PB[q.par][:, :, 0:D]).then_inc(x2_out[q.par], 16)
                sp.dma_start(rows(scratch["tab_b"], q), PB[q.par][:, :, D:2 * D]).then_inc(x2_out[q.par], 16)
            sp.wait_ge(fill_ok, 2)
            groups(sp, body)
            sp.wait_ge(filled, 16 * Q)
            sp.wait_ge(x2_out[0], 48 * ((Q + 1) // 2) + 48)
            sp.wait_ge(x2_out[1], 48 * (Q // 2) + 48)

        @block.gpsimd
        def _(gp):
            gp.sem_inc(g_free, 2)
            gp.memset(mhalf[:, :], -0.5).then_inc(const, 1)
            gp.memset(fill[:, 0:XW - 1], 0.0).then_inc(fill_ok, 1)
            gp.memset(fill[:, XW - 1:XW], float(FAR)).then_inc(fill_ok, 1)
            gp.wait_ge(const, 1)
            gp.wait_ge(zred, 1)
            gp.partition_all_reduce(zm[:, 1:2], zm[:, 0:1], P, REDUCE_MAX).then_inc(zall, 1)
            for i in range(2):
                gp.wait_ge(bn_copied, i + 1)
                gp.tensor_scalar(bn_v[i][:, :], bn_cols[i][:, 4, :], BN_EPS, None, ADD).then_inc(bn_eps, 1)
                gp.wait_ge(bn_eps, i + 1)
                gp.tensor_tensor(bn_v[i][:, :], bn_v[i][:, :], mhalf[:, :], ALU.pow).then_inc(bn_pow, 1)

            def norm(count, b):
                gp.wait_ge(mv_ok, count * GM)
                hold(gp, passed)
                gp.tensor_scalar(ve[b][:, :], mv[b][:, :, 1], LN_EPS, None, ADD).then_inc(ve_ok, 1)
                gp.wait_ge(ve_ok, count)
                gp.tensor_tensor(rs[b][:, :], ve[b][:, :], mhalf[:, 0:GM], ALU.pow).then_inc(rs_ok, 1)

            norm(1, 0)

            def body(q, before, after):
                if before:
                    norm(q.n * 2 + 1, 1)
                if after:
                    norm(q.n * 2 + 2, 0)
            groups(gp, body)
            norm(2 * Q, 1)

        @block.vector
        def _(v):
            nc.vector.tensor_reduce(zm[:, 0:1], k["zmax"][:, :], AX.X, MAX).then_inc(zred, 1)
            for i in range(2):
                v.wait_ge(bn_T, i + 1)
                nc.vector.tensor_copy(bn_cols[i][:, :, :].rearrange("p n c -> p (n c)"), psT[:, 0:5 * NB] if i == 0 else psR[:, 0:5 * NB])\
                    .then_inc(bn_copied, 1)
            for i in range(2):
                v.wait_ge(bn_pow, i + 1)
                v.wait_ge(bn_copied, i + 1)
                nc.vector.tensor_tensor(bn_s[i][:, :], bn_cols[i][:, 1, :], bn_v[i][:, :], MUL).then_inc(bn_sub, 1)
                nc.vector.tensor_tensor(bn_b[i][:, :], bn_cols[i][:, 0, :], bn_cols[i][:, 3, :], SUB).then_inc(bn_sub, 1)
                v.wait_ge(bn_sub, 3 * i + 2)
                nc.vector.tensor_tensor(bn_b[i][:, :], bn_b[i][:, :], bn_s[i][:, :], MUL).then_inc(bn_sub, 1)
                v.wait_ge(bn_sub, 3 * i + 3)
                nc.vector.tensor_tensor(bn_b[i][:, :], bn_b[i][:, :], bn_cols[i][:, 2, :], ADD).then_inc(bn_ok, 1)
            v.wait_ge(zall, 1)
            nc.vector.scalar_tensor_tensor(zm[:, 2:3], zm[:, 1:2], LEAK, zm[:, 1:2], MUL, MAX).then_inc(zlk, 1)
            v.wait_ge(zlk, 1)
            nc.vector.tensor_scalar(corr[:, :, :], k["node"][:, :, H:2 * H], -1.0, zm[:, 2:3], MUL, ADD).then_inc(cdiff, 1)
            v.wait_ge(cexp, 1)
            nc.vector.tensor_scalar(corr[:, :, :], corr[:, :, :], ATT_EPS, None, MUL).then_inc(corr_ok, 1)
            v.wait_ge(corr_ok, 1)
            v.wait_ge(w_in, 48)
            for n in range(len(stages)):
                v.wait_ge(W_high, n + 1)
                stages[n][0].lower(nc, staged(n), *stage_part(n)).then_inc(W_low, 1)

            def low(x, full, ready, at, done):
                v.wait_ge(ready, at)
                x.lower(nc, full[:, :, :]).then_inc(done, 1)

            def low_h1(q, e):
                v.wait_ge(h1_ok, q.n * NX + (e + 3))
                hold(v, passed)
                nc.vector.tensor_copy(h1[e % 2].high[:, :, :], hf1[e % 2][:, :, :]).then_inc(h1_high, 1)
                low(h1[e % 2], hf1[e % 2], h1_high, q.n * NX + (e + 1), h1_low)

            def low_h2(q, e):
                low(h2[e % 2], hf2[e % 2], h2_ok, q.n * NX + (e + 3), h2_low)

            def low_XT(q):
                low(XT[q.par], XF, XT_ok, q.n + 1, XT_low)

            def low_XT2(q):
                low(XT2, XF2, XT2_ok, q.n + 1, XT2_low)

            def moments(src_, count, b):
                for j in range(GM):
                    nc.vector.bn_stats(st[b][:, j, :], src_[:, j, :]).then_inc(st_ok, 1)
                v.wait_ge(st_ok, count * GM)
                hold(v, passed)
                for j in range(GM):
                    nc.vector.bn_aggr(mv[b][:, j, :], st[b][:, j, :]).then_inc(mv_ok, 1)

            def normed(src_, to, count, b):
                v.wait_ge(rs_ok, count)
                for j in range(GM):
                    nc.vector.tensor_scalar(to[:, j, :], src_[:, j, :], mv[b][:, j, 0:1], rs[b][:, j:j + 1], SUB, MUL)\
                        .then_inc(xl_ok, 1)

            def attended(q):
                p = q.par
                v.wait_ge(g_in[p], q.half * 32 + 32)
                nc.vector.tensor_tensor(den[p][:, :, :], U[p][:, :, D:NA], corr[:, bass.ds(q.n * GM, GM), :], ADD)\
                    .then_inc(den_ok, 1)
                nc.vector.tensor_copy(k["deg"][:, bass.ds(q.n * GM, GM)], U[p][:, :, NA]).then_inc(den_ok, 1)
                v.wait_ge(den_ok, q.n * 2 + 2)
                nc.vector.reciprocal(den[p][:, :, :], den[p][:, :, :]).then_inc(rec_ok, 1)
                v.wait_ge(rec_ok, q.n + 1)
                nc.vector.tensor_tensor(
                    U[p][:, :, 0:D].rearrange("p t (h o) -> p t h o", h=H),
                    U[p][:, :, 0:D].rearrange("p t (h o) -> p t h o", h=H),
                    den[p][:, :, :].rearrange("p t (h x) -> p t h x", x=1).to_broadcast([P, GM, H, HD]), MUL)\
                    .then_inc(att_ok, 1)

            def front_start(q, count):
                p = q.par
                v.wait_ge(att_ok, q.n + 1)
                nc.vector.tensor_tensor(R[p][:, :, :], R[p][:, :, :], U[p][:, :, 0:D], ADD).then_inc(x1_ok, 1)
                v.wait_ge(x1_ok, q.n + 1)
                hold(v, passed)
                moments(R[p], count, 0)

            def front_end(q, count):
                normed(R[q.par], XL, count, 0)

            def softmax_start(q):
                p = q.par
                v.wait_ge(lg_ps, q.n + 1)
                nc.vector.tensor_tensor(lg[p][:, :, :], psR[:, 0:GM * NX].rearrange("p (t e) -> p t e", t=GM),
                                        br[:, :].rearrange("p (x e) -> p x e", x=1).to_broadcast([P, GM, NX]), ADD)\
                    .then_inc(lg_ok, 1)
                v.wait_ge(lg_ok, q.n + 1)
                nc.vector.tensor_reduce(lm[p][:, :], lg[p][:, :, :], AX.X, MAX).then_inc(lm_ok, 1)
                v.wait_ge(lm_ok, q.n + 1)
                nc.vector.tensor_tensor(lg[p][:, :, :], lg[p][:, :, :],
                                        lm[p][:, :].rearrange("p (t x) -> p t x", x=1).to_broadcast([P, GM, NX]), SUB)\
                    .then_inc(ls_in, 1)

            def softmax_end(q):
                p = q.par
                v.wait_ge(le_ok, q.n + 1)
                nc.vector.tensor_reduce(ls[p][:, :], lg[p][:, :, :], AX.X, ADD).then_inc(ls_ok, 1)
                v.wait_ge(ls_ok, q.n + 1)
                nc.vector.reciprocal(ls[p][:, :], ls[p][:, :]).then_inc(lr_ok, 1)
                v.wait_ge(lr_ok, q.n + 1)
                nc.vector.tensor_tensor(wg[p][:, :, :], lg[p][:, :, :],
                                        ls[p][:, :].rearrange("p (t x) -> p t x", x=1).to_broadcast([P, GM, NX]), MUL)\
                    .then_inc(wg_ok, 1)

            def start_sum(q):
                p = q.par
                v.wait_ge(x2_out[p], q.half * 48 + 48)
                v.wait_ge(bo_ps, q.n + 1)
                nc.vector.tensor_tensor(acc[p][:, :, :], R[p][:, :, :], psT[:, :].rearrange("p (t f) -> p t f", t=GM), ADD)\
                    .then_inc(acc_ok, 1)
                v.wait_ge(acc_ok, q.n + 1)
                v.sem_inc(g_free, 1)

            def add(q, e):
                p = q.par
                v.wait_ge(y_ps, q.n * NX + (e + 1))
                if e:
                    v.wait_ge(y_ok, q.n * (NX * GM) + (e + 2) * GM)
                for j in range(GM):
                    nc.vector.scalar_tensor_tensor(acc[p][:, j, :], psY[e % 2][:, j * D:(j + 1) * D], wg[p][:, j, e:e + 1],
                                                   acc[p][:, j, :], MUL, ADD).then_inc(y_ok, 1)

            def back_start(q, count):
                v.wait_ge(y_ok, q.n * (NX * GM) + (NX + 2) * GM)
                hold(v, passed)
                moments(acc[q.par], count, 1)

            def back_end(q, count):
                normed(acc[q.par], XL2, count, 1)

            v.sem_inc(y_ok, 2 * GM)
            g0 = Group(0, 0, 0)
            attended(g0)
            front_start(g0, 1)
            front_end(g0, 1)
            low_XT(g0)
            softmax_start(g0)
            softmax_end(g0)

            def body(q, before, after):
                low_h1(q, 0)
                for e in range(NX):
                    if e + 1 < NX:
                        low_h1(q, e + 1)
                    low_h2(q, e)
                    if e == 0:
                        start_sum(q)
                    if e == 1 and before:
                        back_end(q.prev(), q.n * 2 + 1)
                    if e == 3 and before:
                        low_XT2(q.prev())
                    if e == 4 and after:
                        front_end(q.next(), q.n * 2 + 2)
                    if e:
                        add(q, e - 1)
                    elif before:
                        add(q.prev(), NX - 1)
                        back_start(q.prev(), q.n * 2 + 1)
                    if after:
                        if e == 2:
                            attended(q.next())
                        if e == 3:
                            front_start(q.next(), q.n * 2 + 2)
                        if e == 6:
                            low_XT(q.next())
                            softmax_start(q.next())
                        if e == 7:
                            softmax_end(q.next())
            groups(v, body)
            last = Group(Q - 1, (Q - 1) // 2, 0)
            add(last, NX - 1)
            back_start(last, 2 * Q)
            back_end(last, 2 * Q)
            low_XT2(last)

        @block.tensor
        def _(pe):
            pe.wait_ge(bn_in, 160)
            nc.tensor.transpose(psT[:, 0:5 * NB], bn_rows[0][:, :], k["ident"][0:5 * NB, 0:5 * NB]).then_inc(bn_T, 1)
            nc.tensor.transpose(psR[:, 0:5 * NB], bn_rows[1][:, :], k["ident"][0:5 * NB, 0:5 * NB]).then_inc(bn_T, 1)
            pe.wait_ge(w_in, 48)
            pe.wait_ge(bn_copied, 2)
            pe.wait_ge(W_low, len(stages))

            def turn(q, x, count, done):
                pe.wait_ge(xl_ok, count * GM)
                for b in range(KB):
                    for j in range(GM):
                        last = nc.tensor.transpose(psT[:, b * T2 + j * P:b * T2 + (j + 1) * P], x[:, j, b * P:(b + 1) * P],
                                                   k["ident"][:, :])
                last.then_inc(done, 1)

            def router(q):
                pe.wait_ge(XT_ok, q.n + 1)
                for j in range(GM):
                    for b in range(KB):
                        last = nc.tensor.matmul(psR[:, j * NX:(j + 1) * NX], XF[:, b, j * P:(j + 1) * P], Wr[:, b, :],
                                                start=b == 0, stop=b == KB - 1)
                last.then_inc(lg_ps, 1)

            def turn_weights(q):
                pe.wait_ge(wg_ok, q.n + 1)
                for j in range(GM):
                    last = nc.tensor.transpose(psR[0:NX, j * P:(j + 1) * P], wg[q.par][:, j, :], k["ident"][:, :])
                last.then_inc(wT_ps, 1)

            def output_bias(q):
                pe.wait_ge(wT_ok, q.n + 1)
                for j in range(GM):
                    last = nc.tensor.matmul(psT[:, j * D:(j + 1) * D], wT[q.par][:, j, :], bo[:, :], start=True, stop=True)
                last.then_inc(bo_ps, 1)

            def layer1(q, e):
                pe.wait_ge(h1_ok, q.n * NX + (e + 1))
                for m in range(KB):
                    last = products_of(nc, ps1[e % 2][:, m * T2:(m + 1) * T2],
                                       [(W1.at(e, b, slice(m * P, (m + 1) * P)), XT[q.par].at(b)) for b in range(KB)])
                last.then_inc(p1_ok, 1)

            def layer2(q, e):
                pe.wait_ge(h1_ok, q.n * NX + (e + 1) + 2)
                pe.wait_ge(h2_ok, q.n * NX + (e + 1))
                pe.wait_ge(h1_low, q.n * NX + (e + 3))
                for m in range(KB):
                    last = products_of(nc, ps2[e % 2][:, m * T2:(m + 1) * T2],
                                       [(W2.at(e, b, slice(m * P, (m + 1) * P)), h1[e % 2].at(b)) for b in range(KB)])
                last.then_inc(p2_ok, 1)

            def layer3(q, e):
                pe.wait_ge(h2_ok, q.n * NX + (e + 1) + 2)
                pe.wait_ge(y_ok, q.n * (NX * GM) + (e + 1) * GM)
                pe.wait_ge(h2_low, q.n * NX + (e + 3))
                for j in range(GM):
                    last = products_of(nc, psY[e % 2][:, j * D:(j + 1) * D],
                                       [(h2[e % 2].at(b, slice(j * P, (j + 1) * P)), Wo.at(e, b)) for b in range(KB)])
                last.then_inc(y_ps, 1)

            def products(q, j):
                last = products_of(nc, (psR, psT)[j][:, :],
                                   [(XT2.at(b, slice(j * P, (j + 1) * P)), Wg.at(b)) for b in range(KB)])
                last.then_inc(pr_ps, 1)

            g0 = Group(0, 0, 0)
            turn(g0, XL, 1, T_ok)
            router(g0)

            def body(q, before, after):
                pe.wait_ge(XT_low, q.n + 1)
                layer1(q, 0)
                turn_weights(q)
                for e in range(NX):
                    if e + 1 < NX:
                        layer1(q, e + 1)
                    if e == 4 and before:
                        pe.wait_ge(XT2_low, q.n)
                        products(q.prev(), 0)
                        products(q.prev(), 1)
                    layer2(q, e)
                    if e == 2 and before:
                        pe.wait_ge(acc_ok, q.n + 1)
                        turn(q.prev(), XL2, q.n * 2 + 1, T2_ok)
                    if e == 5 and after:
                        if before:
                            pe.wait_ge(pr_ok, q.n * GM)
                        else:
                            pe.wait_ge(acc_ok, 1)
                        turn(q.next(), XL, q.n * 2 + 2, T_ok)
                    if e == 6 and after:
                        router(q.next())
                    if e == 0:
                        output_bias(q)
                    if e:
                        layer3(q, e - 1)
                    elif before:
                        layer3(q.prev(), NX - 1)
            groups(pe, body)
            last = Group(Q - 1, (Q - 1) // 2, 0)
            layer3(last, NX - 1)
            turn(last, XL2, 2 * Q, T2_ok)
            pe.wait_ge(XT2_low, Q)
            products(last, 0)
            products(last, 1)

        @block.scalar
        def _(s):
            s.wait_ge(cdiff, 1)
            nc.scalar.activation(corr[:, :, :], corr[:, :, :], ACT.Exp).then_inc(cexp, 1)
            for n in range(len(stages)):
                s.wait_ge(W_stage[n % 2], 32 * (n // 2 + 1))
                nc.scalar.copy(stages[n][0].at(*stage_part(n))[0], staged(n)).then_inc(W_high, 1)
            s.wait_ge(bn_ok, 2)
            s.sem_inc(h1_ok, 2)
            s.sem_inc(h2_ok, 2)
            s.sem_inc(h1_low, 2)
            s.sem_inc(h2_low, 2)

            def relu(ps, parts, layer, ready, done, lowered, q, e):
                s.wait_ge(ready, q.n * NX + (e + 1))
                s.wait_ge(lowered, q.n * NX + (e + 1))
                for m in range(KB):
                    c = e * KB + m
                    for part in parts:
                        last = nc.scalar.activation(part[:, m, :], ps[e % 2][:, m * T2:(m + 1) * T2], ACT.Relu,
                                                    bias=bn_b[layer][:, c:c + 1], scale=bn_s[layer][:, c:c + 1])
                last.then_inc(done, 1)

            def relu1(q, e):
                relu(ps1, (hf1[e % 2],), 0, p1_ok, h1_ok, h1_low, q, e)

            def relu2(q, e):
                relu(ps2, (h2[e % 2].high, hf2[e % 2]), 1, p2_ok, h2_ok, h2_low, q, e)

            def copy_turned(q, to, full, ready, done):
                s.wait_ge(ready, q.n + 1)
                for part in (to.high, full):
                    last = nc.scalar.copy(part[:, :, :].rearrange("p b t -> p (b t)"), psT[:, :])
                last.then_inc(done, 1)

            def exps(q):
                s.wait_ge(ls_in, q.n + 1)
                nc.scalar.activation(lg[q.par][:, :, :], lg[q.par][:, :, :], ACT.Exp).then_inc(le_ok, 1)

            def copy_weights(q):
                s.wait_ge(wT_ps, q.n + 1)
                nc.scalar.copy(wT[q.par][:, :, :].rearrange("e t p -> e (t p)"), psR[0:NX, 0:T2]).then_inc(wT_ok, 1)

            def copy_products(q):
                s.wait_ge(x2_out[q.par], q.half * 48 + 48)
                for j in range(GM):
                    s.wait_ge(pr_ps, q.n * GM + (j + 1))
                    nc.scalar.copy(PB[q.par][:, j, :], (psR, psT)[j][:, :]).then_inc(pr_ok, 1)

            g0 = Group(0, 0, 0)
            copy_turned(g0, XT[0], XF, T_ok, XT_ok)
            exps(g0)

            def body(q, before, after):
                relu1(q, 0)
                copy_weights(q)
                for e in range(NX):
                    if e + 1 < NX:
                        relu1(q, e + 1)
                    if e == 7 and after:
                        exps(q.next())
                    relu2(q, e)
                    if e == 4 and before:
                        copy_products(q.prev())
                    if e == 2 and before:
                        copy_turned(q.prev(), XT2, XF2, T2_ok, XT2_ok)
                    if e == 5 and after:
                        copy_turned(q.next(), XT[1 - q.par], XF, T_ok, XT_ok)
            groups(s, body)
            last = Group(Q - 1, (Q - 1) // 2, 0)
            copy_turned(last, XT2, XF2, T2_ok, XT2_ok)
            copy_products(last)


def route(nc, a, k, scratch, out, ctx, sem, sbuf, psum):
    pair = range(2)
    Wg = sbuf(ctx, "rWg", [P, KB, NX])
    gb = sbuf(ctx, "rgb", [P, NX])
    bias = sbuf(ctx, "rbias", [P, D])
    rdeg = sbuf(ctx, "rdeg", [P, NT])
    mhalf = sbuf(ctx, "rmhalf", [P, GT])
    tri_f = sbuf(ctx, "tri_f", [P, P])
    tri = sbuf(ctx, "tri", [P, P], BF16)
    ones = sbuf(ctx, "ones", [P, P], BF16)
    e_i = sbuf(ctx, "e_i", [P, NX], I32)
    e_less = sbuf(ctx, "e_less", [P, NX])
    tok_i = sbuf(ctx, "tok_i", [P, GT], I32)
    tok = [sbuf(ctx, f"tok{i}", [P, GT]) for i in pair]
    AG = [sbuf(ctx, f"rAG{i}", [P, GT, D]) for i in pair]
    TP = [sbuf(ctx, f"rTP{i}", [P, GT, D]) for i in pair]
    X2 = [sbuf(ctx, f"rX2{i}", [P, GT, D]) for i in pair]
    XR = [sbuf(ctx, f"rXR{i}", [P, GT, XW]) for i in pair]
    sq = sbuf(ctx, "rsq", [P, D])
    ss = [sbuf(ctx, f"rss{i}", [P, GT]) for i in pair]
    rn = [sbuf(ctx, f"rrn{i}", [P, GT]) for i in pair]
    st = [sbuf(ctx, f"rst{i}", [P, GT, 6]) for i in pair]
    mv = [sbuf(ctx, f"rmv{i}", [P, GT, 2]) for i in pair]
    ve = [sbuf(ctx, f"rve{i}", [P, GT]) for i in pair]
    rs = [sbuf(ctx, f"rrs{i}", [P, GT]) for i in pair]
    xT = [sbuf(ctx, f"rxT{i}", [P, D]) for i in pair]
    lg = sbuf(ctx, "rlg", [P, GT, NX])
    lm = sbuf(ctx, "rlm", [P, GT])
    eq = sbuf(ctx, "req", [P, GT, NX])
    first = sbuf(ctx, "rfirst", [P, GT])
    oh = sbuf(ctx, "roh", [P, GT, NX], BF16)
    before_ = sbuf(ctx, "rbefore", [P, GT + 1, NX], BF16)
    pos = sbuf(ctx, "rpos", [P, GT])
    over = sbuf(ctx, "rover", [P, GT])
    slot = sbuf(ctx, "rslot", [P, GT])
    slot_i = [sbuf(ctx, f"rslot_i{i}", [P, GT], I32) for i in pair]
    cf = sbuf(ctx, "rcf", [1, NX])
    ps_t = [psum(ctx, f"r_ps_t{i}") for i in pair]
    ps_l = psum(ctx, "r_ps_l")
    ps_c = psum(ctx, "r_ps_c")

    def s_(name):
        return sem(ctx, "r_" + name)
    w_in, const, rdeg_ok, tok_ok = map(s_, ("w_in", "const", "rdeg_ok", "tok_ok"))
    g_in = [s_(f"g_in{i}") for i in pair]
    x_out = [s_(f"x_out{i}") for i in pair]
    sent = [sem(ctx, f"r_sent{i}", pool_dma=True) for i in pair]
    g_free, o_ok, ss_ok, rn_ok, xb_ok, x3_ok = map(s_, ("g_free", "o_ok", "ss_ok", "rn_ok", "xb_ok", "x3_ok"))
    st_ok, mv_ok, ve_ok, rs_ok, xl_ok, T_ok, xT_ok, lg_ps = map(s_, (
        "st_ok", "mv_ok", "ve_ok", "rs_ok", "xl_ok", "T_ok", "xT_ok", "lg_ps"))
    dv, le_in, le_ok, oh_ok, cum_ps, slot_ok, pr_ok = map(s_, ("dv", "le_in", "le_ok", "oh_ok", "cum_ps", "slot_ok", "pr_ok"))
    tot_ps, tot_ok, passed = map(s_, ("tot_ps", "tot_ok", "passed"))

    def groups(eng, body):
        for par in range(2):
            body(par, 0, par, False)
        with eng.Fori(1, NG // 2 - 1) as i:
            for par in range(2):
                body(i * 2 + par, i, par, False)
        for par in range(2):
            body(NG - 2 + par, NG // 2 - 1, par, par == 1)

    def rows(dram, g, n=GT):
        return dram[bass.ds(g * (GT * P), n * P), :].rearrange("(t p) f -> p t f", p=P)

    with nc.Block() as block:
        @block.sync
        def _(sp):
            sp.dma_start(Wg[:, :, :], a["L1_ffn_gate_w"].rearrange("(k p) e -> p k e", p=P)).then_inc(w_in, 16)
            sp.dma_start(gb[:, :], a["L1_ffn_gate_b"].rearrange("(x e) -> x e", x=1).to_broadcast([P, NX])).then_inc(w_in, 16)
            sp.dma_start(bias[:, :], a["L1_gnn_bias"].rearrange("(x e) -> x e", x=1).to_broadcast([P, D])).then_inc(w_in, 16)

            def load(g, i, par, last):
                sp.wait_ge(g_free, g + 1)
                sp.dma_start(AG[par][:, :, :], rows(scratch["agg_b"], g)).then_inc(g_in[par], 16)
                sp.dma_start(TP[par][:, :, :], rows(scratch["top_b"], g)).then_inc(g_in[par], 16)
                sp.dma_start(X2[par][:, :, :], rows(scratch["x2"], g)).then_inc(g_in[par], 16)
            groups(sp, load)

        @block.gpsimd
        def _(gp):
            gp.sem_inc(g_free, 2)
            gp.memset(mhalf[:, :], -0.5).then_inc(const, 1)
            gp.memset(ones[:, :], 1.0).then_inc(const, 1)
            gp.memset(tri_f[:, :], 1.0).then_inc(const, 1)
            gp.memset(before_[:, :, :], 0.0).then_inc(const, 1)
            gp.iota(e_i[:, :], [[1, NX]], base=-NX, channel_multiplier=0).then_inc(const, 1)
            gp.iota(tok_i[:, :], [[P, GT]], base=0, channel_multiplier=1).then_inc(const, 1)
            gp.wait_ge(const, 6)
            gp.affine_select(out=tri_f[:, :], in_=tri_f[:, :], compare_op=ALU.is_gt, fill=0.0,
                             base=0, pattern=[[1, P]], channel_multiplier=-1).then_inc(const, 1)

            def body(g, i, par, last):
                gp.wait_ge(g_in[par], i * 48 + 48)
                gp.tensor_tensor(X2[par][:, :, :], X2[par][:, :, :],
                                 bias[:, :].rearrange("p (x f) -> p x f", x=1).to_broadcast([P, GT, D]), ADD)\
                    .then_inc(xb_ok, 1)
                gp.wait_ge(ss_ok, g * GT + GT + 1)
                gp.tensor_tensor(rn[par][:, :], ss[par][:, :], mhalf[:, :], ALU.pow).then_inc(rn_ok, 1)
                gp.wait_ge(mv_ok, g * GT + GT)
                hold(gp, passed)
                gp.tensor_scalar(ve[par][:, :], mv[par][:, :, 1], LN_EPS, None, ADD).then_inc(ve_ok, 1)
                gp.wait_ge(ve_ok, g + 1)
                gp.tensor_tensor(rs[par][:, :], ve[par][:, :], mhalf[:, :], ALU.pow).then_inc(rs_ok, 1)
                gp.wait_ge(slot_ok, g + 1)
                gp.wait_ge(pr_ok, g * 2 + 2)
                hold(gp, passed)
                for j in range(GT):
                    gp.indirect_dma_start(out=scratch["buf"], out_offset=bass.IndirectOffsetOnAxis(ap=slot_i[par][:, j:j + 1], axis=0),
                                          in_=XR[par][:, j, :], in_offset=None,
                                          bounds_check=NX * SLOTS - 1, oob_is_err=False).then_inc(sent[par], 16)
            gp.wait_ge(w_in, 48)
            groups(gp, body)
            for par in pair:
                gp.wait_ge(sent[par], 16 * GT * (NG // 2))

        @block.vector
        def _(v):
            v.wait_ge(const, 7)
            nc.vector.tensor_copy(tri[:, :], tri_f[:, :]).then_inc(tok_ok, 1)
            nc.vector.tensor_copy(e_less[:, :], e_i[:, :]).then_inc(tok_ok, 1)
            nc.vector.tensor_scalar(rdeg[:, :], k["deg"][:, :], 1.0, None, MAX).then_inc(rdeg_ok, 1)
            for par in pair:
                nc.vector.tensor_scalar(tok[par][:, :], tok_i[:, :], float((par - 2) * GT * P), None, ADD).then_inc(tok_ok, 1)
            v.wait_ge(rdeg_ok, 1)
            nc.vector.reciprocal(rdeg[:, :], rdeg[:, :]).then_inc(rdeg_ok, 1)
            v.wait_ge(rdeg_ok, 2)
            v.wait_ge(w_in, 48)
            v.wait_ge(tok_ok, 4)
            v.sem_inc(oh_ok, 1)

            def body(g, i, par, last):
                v.wait_ge(g_in[par], i * 48 + 48)
                for j in range(GT):
                    nc.vector.scalar_tensor_tensor(AG[par][:, j, :], AG[par][:, j, :], rdeg[:, bass.ds(g * GT + j, 1)],
                                                   TP[par][:, j, :], MUL, ADD).then_inc(o_ok, 1)
                v.wait_ge(rn_ok, g + 1)
                v.wait_ge(xb_ok, g + 1)
                v.wait_ge(x_out[par], i * 16 + 16)
                if not (isinstance(i, int) and i == 0):
                    v.wait_ge(sent[par], i * (16 * GT))
                for j in range(GT):
                    nc.vector.scalar_tensor_tensor(XR[par][:, j, D:2 * D], AG[par][:, j, :], rn[par][:, j:j + 1],
                                                   X2[par][:, j, :], MUL, ADD).then_inc(x3_ok, 1)
                v.wait_ge(x3_ok, g * GT + GT)
                v.sem_inc(g_free, 1)
                for j in range(GT):
                    nc.vector.bn_stats(st[par][:, j, :], XR[par][:, j, D:2 * D]).then_inc(st_ok, 1)
                v.wait_ge(st_ok, g * GT + GT)
                hold(v, passed)
                for j in range(GT):
                    nc.vector.bn_aggr(mv[par][:, j, :], st[par][:, j, :]).then_inc(mv_ok, 1)
                nc.vector.tensor_scalar(tok[par][:, :], tok[par][:, :], float(2 * GT * P), None, ADD).then_inc(pr_ok, 1)
                v.wait_ge(rs_ok, g + 1)
                for j in range(GT):
                    nc.vector.tensor_scalar(XR[par][:, j, 0:D], XR[par][:, j, D:2 * D], mv[par][:, j, 0:1],
                                            rs[par][:, j:j + 1], SUB, MUL).then_inc(xl_ok, 1)

                def wide(x):
                    return x.rearrange("p (t x) -> p t x", x=1).to_broadcast([P, GT, NX])

                def less():
                    return e_less[:, :].rearrange("p (x e) -> p x e", x=1).to_broadcast([P, GT, NX])
                STEPS = 14
                n = [0]

                def step(ins):
                    n[0] += 1
                    ins.then_inc(dv, 1)
                    v.wait_ge(dv, g * STEPS + n[0])
                v.wait_ge(lg_ps, g + 1)
                step(nc.vector.tensor_tensor(lg[:, :, :], ps_l[:, 0:GT * NX].rearrange("p (t e) -> p t e", t=GT),
                                             gb[:, :].rearrange("p (x e) -> p x e", x=1).to_broadcast([P, GT, NX]), ADD))
                step(nc.vector.tensor_reduce(lm[:, :], lg[:, :, :], AX.X, MAX))
                nc.vector.tensor_tensor(lg[:, :, :], lg[:, :, :], wide(lm[:, :]), SUB).then_inc(le_in, 1)
                v.wait_ge(le_ok, g + 1)
                step(nc.vector.tensor_reduce(lm[:, :], lg[:, :, :], AX.X, ADD))
                step(nc.vector.reciprocal(lm[:, :], lm[:, :]))
                step(nc.vector.tensor_tensor(lg[:, :, :], lg[:, :, :], wide(lm[:, :]), MUL))
                step(nc.vector.tensor_reduce(lm[:, :], lg[:, :, :], AX.X, MAX))
                step(nc.vector.tensor_tensor(eq[:, :, :], lg[:, :, :], wide(lm[:, :]), ALU.is_equal))
                step(nc.vector.tensor_tensor(eq[:, :, :], eq[:, :, :], less(), MUL))
                step(nc.vector.tensor_reduce(first[:, :], eq[:, :, :], AX.X, MIN))
                step(nc.vector.tensor_tensor(oh[:, :, :], less(), wide(first[:, :]), ALU.is_equal))
                for j in range(GT):
                    v.wait_ge(oh_ok, g * (GT + 1) + j + 1)
                    nc.vector.tensor_tensor(before_[:, j + 1, :], before_[:, j, :], oh[:, j, :], ADD).then_inc(oh_ok, 1)
                v.wait_ge(pr_ok, g * 2 + 1)
                nc.vector.tensor_copy(XR[par][:, :, 2 * D], lm[:, :]).then_inc(pr_ok, 1)
                nc.vector.tensor_copy(XR[par][:, :, 2 * D + 1], tok[par][:, :]).then_inc(tok_ok, 1)
                v.wait_ge(cum_ps, g + 1)
                step(nc.vector.tensor_tensor(eq[:, :, :], ps_c[:, 0:GT * NX].rearrange("p (t e) -> p t e", t=GT),
                                             oh[:, :, :], MUL))
                nc.vector.tensor_copy(before_[:, 0, :], before_[:, GT, :]).then_inc(oh_ok, 1)
                step(nc.vector.tensor_reduce(pos[:, :], eq[:, :, :], AX.X, ADD))
                step(nc.vector.tensor_scalar(over[:, :], pos[:, :], float(CAP), float(FAR), ALU.is_ge, MUL))
                step(nc.vector.scalar_tensor_tensor(pos[:, :], pos[:, :], float(NX * SLOTS), over[:, :], ADD, ADD))
                v.wait_ge(tok_ok, g + 5)
                nc.vector.scalar_tensor_tensor(slot_i[par][:, :], first[:, :], float(SLOTS), pos[:, :], MUL, ADD)\
                    .then_inc(slot_ok, 1)
            groups(v, body)

            v.wait_ge(tot_ps, 1)
            nc.vector.tensor_scalar(cf[:, :], ps_l[0:1, 0:NX], float(CAP), 1.0 / TC, MIN, MUL).then_inc(tot_ok, 1)
            v.wait_ge(tot_ok, 1)
            nc.vector.tensor_scalar(cf[:, :], cf[:, :], 0.5 - 0.5 / TC, None, ADD).then_inc(tot_ok, 1)
            v.wait_ge(tot_ok, 2)
            nc.vector.tensor_scalar(k["chunks"][:, :], cf[:, :], 1.0, None, MAX).then_inc(tot_ok, 1)

        @block.tensor
        def _(pe):
            pe.wait_ge(w_in, 48)
            pe.wait_ge(tok_ok, 4)

            def body(g, i, par, last):
                for j in range(GT + 1):
                    if j < GT:
                        pe.wait_ge(xl_ok, g * GT + (j + 1))
                        if j >= 2:
                            pe.wait_ge(xT_ok, g * GT + (j - 1))
                        for b in range(KB):
                            last_i = nc.tensor.transpose(ps_t[j % 2][:, b * P:(b + 1) * P],
                                                         XR[par][:, j, b * P:(b + 1) * P], k["ident"][:, :])
                        last_i.then_inc(T_ok, 1)
                    if j:
                        pe.wait_ge(xT_ok, g * GT + j)
                        for b in range(KB):
                            last_i = nc.tensor.matmul(ps_l[:, (j - 1) * NX:j * NX], xT[(j - 1) % 2][:, b * P:(b + 1) * P],
                                                      Wg[:, b, :], start=b == 0, stop=b == KB - 1)
                last_i.then_inc(lg_ps, 1)
                pe.wait_ge(oh_ok, g * (GT + 1) + GT + 1)
                nc.tensor.matmul(ps_c[:, 0:GT * NX], tri[:, :], oh[:, :, :].rearrange("p t e -> p (t e)"),
                                 start=True, stop=False)
                nc.tensor.matmul(ps_c[:, 0:GT * NX], ones[:, :], before_[:, 0:GT, :].rearrange("p t e -> p (t e)"),
                                 start=False, stop=True).then_inc(cum_ps, 1)
            groups(pe, body)
            pe.wait_ge(oh_ok, NG * (GT + 1) + 1)
            nc.tensor.matmul(ps_l[0:1, 0:NX], ones[:, 0:1], before_[:, 0, :], start=True, stop=True).then_inc(tot_ps, 1)

        @block.scalar
        def _(s):
            s.sem_inc(ss_ok, 1)
            for par in pair:
                first_turn(s, k, x_out[par])

            def body(g, i, par, last):
                for j in range(GT):
                    s.wait_ge(o_ok, g * GT + (j + 1))
                    s.wait_ge(ss_ok, g * GT + (j + 1))
                    nc.scalar.activation(sq[:, :], AG[par][:, j, :], ACT.Square, accum_out=ss[par][:, j:j + 1])\
                        .then_inc(ss_ok, 1)
                s.wait_ge(x3_ok, g * GT + GT)
                if not last:
                    s.dma_start(rows(out, g), XR[par][:, :, D:2 * D]).then_inc(x_out[par], 16)
                else:
                    s.dma_start(rows(out, g, GT - 1), XR[par][:, 0:GT - 1, D:2 * D]).then_inc(x_out[par], 16)
                    s.dma_start(out[(NT - 1) * P:N, :], XR[par][0:TAIL, GT - 1, D:2 * D]).then_inc(x_out[par], 16)
                for j in range(GT):
                    s.wait_ge(T_ok, g * GT + (j + 1))
                    nc.scalar.copy(xT[j % 2][:, :], ps_t[j % 2][:, 0:D]).then_inc(xT_ok, 1)
                s.wait_ge(le_in, g + 1)
                nc.scalar.activation(lg[:, :, :], lg[:, :, :], ACT.Exp).then_inc(le_ok, 1)
            groups(s, body)
            s.wait_ge(x_out[0], 16 * (NG // 2 + 1))
            s.wait_ge(x_out[1], 16 * (NG // 2 + 2))


def experts(nc, a, k, scratch, out, ctx, sem, sbuf, psum):
    pair = range(2)
    w1 = [sbuf(ctx, f"xw1{i}", [P, KB, FH]) for i in pair]
    w2 = [sbuf(ctx, f"xw2{i}", [P, FB, D]) for i in pair]
    b2 = [sbuf(ctx, f"xb2{i}", [P, D]) for i in pair]
    b1r = sbuf(ctx, "xb1r", [NX * FB, P])
    b1T = sbuf(ctx, "xb1T", [P, NX * FB])
    b1 = [sbuf(ctx, f"xb1{i}", [P, FB]) for i in pair]
    XN = sbuf(ctx, "xXN", [P, CT, D])
    XB = sbuf(ctx, "xXB", [P, CT, XW - D])
    xT = sbuf(ctx, "xxT", [P, KB, TC])
    hid = sbuf(ctx, "xhid", [P, FB, TC])
    Y = sbuf(ctx, "xY", [P, CT, D])
    C = sbuf(ctx, "xC", [P, CT, D])
    Z = sbuf(ctx, "xZ", [P, CT, D])
    odd = sbuf(ctx, "xodd", [P, CT, D], I32)
    num = sbuf(ctx, "xnum", [P, CT, D])
    YR = sbuf(ctx, "xYR", [P, CT, D])
    tok = sbuf(ctx, "xtok", [P, CT], I32)
    ps_t = [psum(ctx, f"x_ps_t{i}") for i in pair]
    ps_h = [psum(ctx, f"x_ps_h{i}") for i in pair]
    ps_y = [psum(ctx, f"x_ps_y{i}") for i in pair]

    def s_(name):
        return sem(ctx, "x_" + name)
    b_in, b_T, b_ok, bc_ok = map(s_, ("b_in", "b_T", "b_ok", "bc_ok"))
    w_in = [s_(f"w_in{i}") for i in pair]
    n_in, n_free, r_in, r_free = map(s_, ("n_in", "n_free", "r_in", "r_free"))
    T_ok, xT_ok, h_ps, h_ok, y_ps, y_ok = map(s_, ("T_ok", "xT_ok", "h_ps", "h_ok", "y_ps", "y_ok"))
    dv, row_ok, row_free, passed = map(s_, ("dv", "row_ok", "row_free", "passed"))
    sent = sem(ctx, "x_sent", pool_dma=True)
    STEPS = 8

    def all_experts(eng, name, before, chunk, after):
        done = eng.alloc_register(name)
        eng.reg_mov(done, 0)
        row = eng.alloc_register(name + "_row")

        def one(e, i, par, last):
            count = eng.value_load(k["chunks"][0:1, bass.ds(e, 1)], min_val=1, max_val=SLOTS // TC)
            g = eng.snap(done, min_val=0, max_val=NX * SLOTS // TC)
            before(e, i, par, g)
            eng.reg_mov(row, e * SLOTS)
            with eng.Fori(0, count):
                g = eng.snap(done, min_val=0, max_val=NX * SLOTS // TC)
                chunk(g, eng.snap(row, min_val=0, max_val=(NX * SLOTS // TC - 1) * TC), par)
                eng.reg_add(done, done, 1)
                eng.reg_add(row, row, TC)
            if not last:
                after(e, i, par, eng.snap(done, min_val=0, max_val=NX * SLOTS // TC))
        with eng.Fori(0, NX // 2 - 1) as i:
            for par in range(2):
                one(i * 2 + par, i, par, False)
        for par in range(2):
            one(NX - 2 + par, NX // 2 - 1, par, True)
        return done

    def nothing(*args):
        pass

    with nc.Block() as block:
        @block.sync
        def _(sp):
            def chunk(g, row, par):
                rows = scratch["buf"][bass.ds(row, TC), :].rearrange("(t p) f -> p t f", p=P)
                sp.wait_ge(n_free, g + 1)
                sp.dma_start(XN[:, :, :], rows[:, :, 0:D]).then_inc(n_in, 16)
                sp.wait_ge(r_free, g + 1)
                sp.dma_start(XB[:, :, :], rows[:, :, D:XW]).then_inc(r_in, 16)
            all_experts(sp, "x_sp", nothing, chunk, nothing)

        @block.gpsimd
        def _(gp):
            gp.sem_inc(row_free, 1)

            def chunk(g, row, par):
                gp.wait_ge(row_ok, g + 1)
                hold(gp, passed)
                for j in range(CT):
                    gp.indirect_dma_start(out=out, out_offset=bass.IndirectOffsetOnAxis(ap=tok[:, j:j + 1], axis=0),
                                          in_=YR[:, j, :], in_offset=None,
                                          bounds_check=N - 1, oob_is_err=False).then_inc(sent, 16)
                gp.wait_ge(sent, g * (16 * CT) + 16 * CT)
                gp.sem_inc(row_free, 1)
            all_experts(gp, "x_pool", nothing, chunk, nothing)

        @block.vector
        def _(v):
            v.sem_inc(r_free, 1)
            v.sem_inc(y_ok, 2)
            v.wait_ge(b_T, 1)
            nc.vector.tensor_copy(b1T[:, :], ps_t[0][:, 0:NX * FB]).then_inc(b_ok, 1)

            def before(e, i, par, g):
                v.wait_ge(w_in[par], i * 48 + 48)
                hold(v, passed)

            def chunk(g, row, par):
                n = [0]

                def step(ins):
                    n[0] += 1
                    ins.then_inc(dv, 1)
                    v.wait_ge(dv, g * STEPS + n[0])
                v.wait_ge(r_in, g * 16 + 16)
                for j in range(CT):
                    v.wait_ge(y_ps, g * CT + (j + 1))
                    nc.vector.tensor_tensor(Y[:, j, :], ps_y[j % 2][:, 0:D], b2[par][:, :], ADD).then_inc(y_ok, 1)
                v.wait_ge(y_ok, g * CT + CT + 2)
                step(nc.vector.tensor_tensor(Y[:, :, :], Y[:, :, :], XB[:, :, D:D + 1].to_broadcast([P, CT, D]), MUL))
                step(nc.vector.tensor_scalar(C[:, :, :], Y[:, :, :], -BIGGEST, BIGGEST, MAX, MIN))
                step(nc.vector.tensor_tensor(odd[:, :, :], C[:, :, :], Y[:, :, :], ALU.not_equal))
                step(nc.vector.tensor_tensor(num[:, :, :], Y[:, :, :], Y[:, :, :], ALU.is_equal))
                step(nc.vector.tensor_scalar(Z[:, :, :], C[:, :, :], -NN_INF, NN_INF, MAX, MIN))
                step(nc.vector.tensor_tensor(Z[:, :, :], Z[:, :, :], num[:, :, :], MUL))
                hold(v, passed)
                step(nc.vector.copy_predicated(C[:, :, :], odd[:, :, :], Z[:, :, :]))
                v.wait_ge(row_free, g + 1)
                step(nc.vector.tensor_copy(tok[:, :], XB[:, :, D + 1]))
                nc.vector.tensor_tensor(YR[:, :, :], C[:, :, :], XB[:, :, 0:D], ADD).then_inc(row_ok, 1)
                v.wait_ge(row_ok, g + 1)
                v.sem_inc(r_free, 1)
            all_experts(v, "x_dve", before, chunk, nothing)

        @block.tensor
        def _(pe):
            pe.sem_inc(n_free, 1)
            pe.wait_ge(b_in, 16)
            nc.tensor.transpose(ps_t[0][:, 0:NX * FB], b1r[:, :], k["ident"][0:NX * FB, 0:NX * FB]).then_inc(b_T, 1)
            pe.wait_ge(b_ok, 1)

            def before(e, i, par, g):
                pe.wait_ge(w_in[par], i * 48 + 48)
                hold(pe, passed)

            def chunk(g, row, par):
                pe.wait_ge(n_in, g * 16 + 16)
                for b in range(KB):
                    for j in range(CT):
                        last = nc.tensor.transpose(ps_t[b][:, j * P:(j + 1) * P], XN[:, j, b * P:(b + 1) * P], k["ident"][:, :])
                    last.then_inc(T_ok, 1)
                pe.wait_ge(T_ok, g * KB + KB)
                pe.sem_inc(n_free, 1)
                pe.wait_ge(xT_ok, g * KB + KB)
                for m in range(FB):
                    pe.wait_ge(h_ok, g * FB + (m + 1))
                    for b in range(KB):
                        last = nc.tensor.matmul(ps_h[m % 2][:, :], w1[par][:, b, m * P:(m + 1) * P], xT[:, b, :],
                                                start=b == 0, stop=b == KB - 1)
                    last.then_inc(h_ps, 1)
                pe.wait_ge(h_ok, g * FB + FB + 2)
                for j in range(CT):
                    pe.wait_ge(y_ok, g * CT + (j + 1))
                    for b in range(FB):
                        last = nc.tensor.matmul(ps_y[j % 2][:, 0:D], hid[:, b, j * P:(j + 1) * P], w2[par][:, b, :],
                                                start=b == 0, stop=b == FB - 1)
                    last.then_inc(y_ps, 1)

            all_experts(pe, "x_pe", before, chunk, nothing)

        @block.scalar
        def _(s):
            s.sem_inc(h_ok, 2)
            s.dma_start(b1r[:, :], a["L1_ffn_b1"].rearrange("e (m p) -> (e m) p", p=P)).then_inc(b_in, 16)

            def load(e, par):
                s.dma_start(w1[par][:, :, :], a["L1_ffn_w1"][bass.ds(e, 1), :, :].rearrange("x (k p) f -> p (x k) f", p=P))\
                    .then_inc(w_in[par], 16)
                s.dma_start(w2[par][:, :, :], a["L1_ffn_w2"][bass.ds(e, 1), :, :].rearrange("x (m p) f -> p (x m) f", p=P))\
                    .then_inc(w_in[par], 16)
                s.dma_start(b2[par][:, :], a["L1_ffn_b2"][bass.ds(e, 1), :].to_broadcast([P, D])).then_inc(w_in[par], 16)
            load(0, 0)
            load(1, 1)
            s.wait_ge(b_ok, 1)

            def before(e, i, par, g):
                s.wait_ge(h_ok, g * FB + 2)
                hold(s, passed)
                nc.scalar.copy(b1[par][:, :], b1T[:, bass.ds(e * FB, FB)]).then_inc(bc_ok, 1)
                s.wait_ge(bc_ok, e + 1)

            def chunk(g, row, par):
                for b in range(KB):
                    s.wait_ge(T_ok, g * KB + (b + 1))
                    nc.scalar.copy(xT[:, b, :], ps_t[b][:, :]).then_inc(xT_ok, 1)
                for m in range(FB):
                    s.wait_ge(h_ps, g * FB + (m + 1))
                    nc.scalar.activation(hid[:, m, :], ps_h[m % 2][:, :], ACT.Relu, bias=b1[par][:, m:m + 1])\
                        .then_inc(h_ok, 1)

            def after(e, i, par, g):
                s.wait_ge(y_ok, g * CT + 2)
                hold(s, passed)
                load(e + 2, par)
            all_experts(s, "x_act", before, chunk, after)


_INS = ["x", "src", "dst", "L0_gnn_W", "L0_gnn_a_src", "L0_gnn_a_dst",
        "L0_ffn_Wr", "L0_ffn_br", "L0_ffn_W1", "L0_ffn_b1", "L0_ffn_g1", "L0_ffn_be1", "L0_ffn_m1", "L0_ffn_v1",
        "L0_ffn_W2", "L0_ffn_b2", "L0_ffn_g2", "L0_ffn_be2", "L0_ffn_m2", "L0_ffn_v2", "L0_ffn_Wo", "L0_ffn_bo",
        "L1_gnn_weight", "L1_gnn_bias", "L1_ffn_gate_w", "L1_ffn_gate_b",
        "L1_ffn_w1", "L1_ffn_b1", "L1_ffn_w2", "L1_ffn_b2"]
_SCRATCH = {"tab_a": (NP, NA), "resid_a": (NP, D), "agg_a": (NP, NV), "x2": (NP, D), "top_b": (NP, D),
            "tab_b": (NP, D), "agg_b": (NP, D), "buf": (NT // GM * FILL * P, XW),
            "void": (VOID, 16)}
_INT_SCRATCH = {"src_p": (EROWS * P,), "dst_p": (EROWS * P,)}


def kernel(**inputs):
    import numpy as _np
    import concourse.bacc as _bacc
    from concourse.bass_utils import run_bass_kernel_spmd as _run

    nc = _bacc.Bacc("TRN2", target_bir_lowering=False, num_devices=1)
    arrays, args = {}, {}
    for name in _INS:
        x = _np.ascontiguousarray(inputs[name])
        arrays[f"in_{name}_dram"] = x
        args[name] = nc.dram_tensor(f"in_{name}_dram", x.shape, mybir.dt.from_np(x.dtype), kind="ExternalInput").ap()
    scratch = {n: nc.dram_tensor(n, s, FP32, kind="Internal").ap() for n, s in _SCRATCH.items()}
    scratch.update({n: nc.dram_tensor(n, s, I32, kind="Internal").ap() for n, s in _INT_SCRATCH.items()})
    out = nc.dram_tensor("out_0_dram", (N, D), FP32, kind="ExternalOutput").ap()
    build(nc, args, out, scratch)
    r = _run(nc, [arrays], core_ids=[0])
    return r.results[0]["out_0_dram"]
```
